# Optimizing a Trainium2 kernel written in Bass

```python
import numpy as np
import jax
import jax.numpy as jnp

def _softmax(x, axis=-1):
    return jax.nn.softmax(x, axis=axis)

def _gelu(x):
    return jax.nn.gelu(x, approximate=True)

def _silu(x):
    return jax.nn.silu(x)

def _sigmoid(x):
    return jax.nn.sigmoid(x)

def _layernorm(x, axis=-1, eps=1e-05):
    m = jnp.mean(x, axis=axis, keepdims=True)
    v = jnp.var(x, axis=axis, keepdims=True)
    return (x - m) / jnp.sqrt(v + eps)

def _scatter_add(tgt, idx, src, axis=0):
    return tgt.at[idx].add(src)

def _segment_sum(src, seg, n):
    return jax.ops.segment_sum(src, seg, n)
kernel_name = 'mk_flamingo_gated_d1_seqx_r2_96e7a1'

def setup_inputs(seed: int=0):
    np.random.seed(seed)
    _w = jnp.asarray

    def _rec_inputs():
        import jax
        import jax.numpy as jnp
        _rk = jax.random.key(seed)
        x = -7.109e-05 + 0.9999 * jax.random.normal(jax.random.fold_in(_rk, 1), (4, 1024, 2048), jnp.float32)
        _lenS = 1024 - jax.random.randint(jax.random.fold_in(_rk, 7), (4,), 0, max(1, 1024 // 4) + 1, jnp.int32)
        _lenS2 = 64 - jax.random.randint(jax.random.fold_in(_rk, 8), (4,), 0, max(1, 64 // 4) + 1, jnp.int32)
        _ctx_4096P = jax.random.normal(jax.random.fold_in(_rk, 11), (4, 16, 2048), jnp.float32)
        _ctx_4096c = jax.random.dirichlet(jax.random.fold_in(_rk, 511), 0.3 * jnp.ones((16,), jnp.float32), (4, 64))
        _ctx_4096t = jnp.einsum('bsk,bkd->bsd', _ctx_4096c, _ctx_4096P)
        _ctx_4096t = _ctx_4096t * jax.lax.rsqrt(jnp.mean(jnp.square(_ctx_4096t)) + 1e-12) * 0.953939
        ctx_4096 = -0.00010331 + 0.999899 * (_ctx_4096t + 0.3 * jax.random.normal(jax.random.fold_in(_rk, 611), (4, 64, 2048), jnp.float32))
        _g = jax.random.normal(jax.random.fold_in(_rk, 9001), (2, 1), jnp.float32)
        _g = jnp.sign(_g) * jnp.maximum(jnp.abs(_g), 1.0) + (_g == 0) * 1.0
        g_xattn = _g[0]
        g_ffn = _g[1]
        return (x, ctx_4096, g_xattn, g_ffn)
    x, ctx_4096, g_xattn, g_ffn = _rec_inputs()

    def _L0_xattn_setup():
        import jax, jax.numpy as jnp
        import numpy as np
        key = jax.random.key(seed)
        k1, k2 = jax.random.split(key)
        B, Lq, Lk, D = (16, 512, 1024, 2048)
        query = jax.random.normal(k1, (B, Lq, D), dtype=jnp.float32)
        key_t = jax.random.normal(k2, (B, Lk, D), dtype=jnp.float32)
        return {'query': query, 'key': key_t}
    _L0_xattn_all = _L0_xattn_setup()
    _L0_xattn_in = {k: v for k, v in _L0_xattn_all.items() if k in ()}
    del _L0_xattn_all

    def _L0_ffn_setup():
        import jax, jax.numpy as jnp
        import numpy as np

        def binarize_weight(W):
            alpha = jnp.mean(jnp.abs(W), axis=tuple(range(1, W.ndim)), keepdims=True)
            return alpha * jnp.sign(W)
        key = jax.random.key(seed)
        k1, k2, k3 = jax.random.split(key, 3)
        B, S, D_IN, D_OUT = (4, 1024, 2048, 2048)
        x = jax.random.normal(k1, (B, S, D_IN), dtype=jnp.float32)
        weight_real = jax.random.normal(k2, (D_OUT, D_IN), dtype=jnp.float32)
        bias = jax.random.normal(k3, (D_OUT,), dtype=jnp.float32)
        return {'x': x, 'weight_real': weight_real, 'bias': bias}
    _L0_ffn_all = _L0_ffn_setup()
    _L0_ffn_in = {k: v for k, v in _L0_ffn_all.items() if k in ('weight_real', 'bias')}
    del _L0_ffn_all
    return {'x': x, 'ctx_4096': ctx_4096, 'g_xattn': g_xattn, 'g_ffn': g_ffn, 'L0_ffn_weight_real': _L0_ffn_in['weight_real'], 'L0_ffn_bias': _L0_ffn_in['bias']}

def reference(x, ctx_4096, g_xattn, g_ffn, L0_ffn_weight_real, L0_ffn_bias):
    import jax
    import jax.numpy as jnp

    def _L0_xattn_ref(query, key):
        import jax, jax.numpy as jnp
        import numpy as np
        a = jnp.einsum('bqd,bkd->bqk', query, key)
        e = jax.nn.softmax(a, axis=-1)
        c = jnp.einsum('bqk,bkd->bqd', e, key)
        return c

    def _L0_ffn_ref(x, weight_real, bias):
        import jax, jax.numpy as jnp
        import numpy as np

        def binarize_weight(W):
            alpha = jnp.mean(jnp.abs(W), axis=tuple(range(1, W.ndim)), keepdims=True)
            return alpha * jnp.sign(W)
        W = binarize_weight(weight_real)
        return jnp.einsum('bsi,oi->bso', x, W) + bias
    x = x + jnp.tanh(g_xattn[0]) * _L0_xattn_ref(_layernorm(x, axis=-1), ctx_4096)
    x = x + jnp.tanh(g_ffn[0]) * _L0_ffn_ref(_layernorm(x, axis=-1), L0_ffn_weight_real, L0_ffn_bias)
    return x

_drawn_inputs = setup_inputs


def setup_inputs(seed=0):
    import zlib

    import numpy as np

    out = dict(_drawn_inputs(seed))
    spreads = {}
    factors = {}
    for name, (base, spread) in spreads.items():
        noise = np.random.default_rng([zlib.crc32(name.encode()), seed]).standard_normal(out[name].shape)
        drawn = base * np.exp(spread * noise) if base else spread * noise
        out[name] = jnp.asarray(drawn.astype(out[name].dtype))
    for name, factor in factors.items():
        out[name] = (out[name] * factor).astype(out[name].dtype)
    return out
```

```python
import concourse.bass as bass
from concourse import mybir
from contextlib import ExitStack

P = 128
BANK = 512
GROUP = BANK // P
LN_SCALE = 2.0 ** 10
PROB_SCALE = 2.0 ** 14
KEY_TOP = 2.0 ** 14
EPS = 1e-5


def flamingo_gated_kernel(
    nc: bass.Bass,
    x: bass.AP,
    ctx_keys: bass.AP,
    g_xattn: bass.AP,
    g_ffn: bass.AP,
    weight: bass.AP,
    bias: bass.AP,
    out: bass.AP,
):
    F32, F16, I32 = mybir.dt.float32, mybir.dt.float16, mybir.dt.int32
    ALU = mybir.AluOpType
    ACT = mybir.ActivationFunctionType
    X = mybir.AxisListType.X

    NB, S, D = x.shape
    NKEY = ctx_keys.shape[1]
    DO = weight.shape[0]
    NT = NB * S // P
    ND = D // P
    NC = D // BANK
    NG = ND // GROUP
    NW = DO // P
    TILES_PER_BATCH = S // P
    RX, RW = 4, 3
    STEPS = 4
    LOOPS = (NT - 4) // STEPS
    BLOCKS = 16
    assert NKEY * 2 == P and D == DO and NC == 4 and NG == 4 and NB == 4
    assert TILES_PER_BATCH == 2 * STEPS and NT == 4 + STEPS * LOOPS

    x_t = x.rearrange("b (t p) d -> (b t) p d", p=P)
    out_t = out.rearrange("b (t p) d -> (b t) p d", p=P)
    ctx_t = ctx_keys.rearrange("(i b) k d -> i (b k) d", b=2)
    w_t = weight.rearrange("(t p) d -> t p d", p=P)

    X1T_AT = {0: [0, 1], 1: [2], 2: [3]}
    XT_AT = {4: 0, 5: 1, 6: 2, 7: 3}
    SCORES_AT, PT_AT = 8, 10
    C_AT = {11: 0, 12: 1, 13: 2, 14: 3}
    PAIR_XT = {4: (2, 0), 5: (2, 1), 6: (2, 2), 7: (2, 3), 16: (3, 0), 17: (3, 1), 18: (3, 2), 19: (3, 3)}
    PAIR_SCORES = {8: 2, 20: 3}
    PAIR_PT = {10: 2, 22: 3}
    PAIR_C = {11: (2, 0), 12: (2, 1), 13: (2, 2), 14: (2, 3), 23: (3, 0), 24: (3, 1), 25: (3, 2), 26: (3, 3)}
    PAIR_X1T = {28: [0, 1], 29: [2], 30: [3]}
    PAIR_ALPHA = {7: 1, 15: 2, 23: 3}
    PAIR_BLOCKS = 32

    def seq_xT(u):
        return {0: 0, 1: 12, 2: 24, 3: 28}[u] if isinstance(u, int) and u < 4 else u * 8 + 8

    def seq_x1T(u):
        return {0: 16, 1: 20, 2: 32}[u] if isinstance(u, int) and u < 3 else u * 8 + 12

    SEQ_KEYS = 4

    def seq_y(t, n):
        return 2 * n + t if isinstance(t, int) and t < 2 else t * 4 + n

    with ExitStack() as ctx:
        def sb(name, shape, dt=F32):
            return ctx.enter_context(nc.sbuf_tensor(name, shape, dt))

        def psum(name, shape):
            return ctx.enter_context(nc.psum_tensor(name, shape, F32))

        def sem(name):
            return ctx.enter_context(nc.semaphore(name))

        kt_dram = nc.dram_tensor("kt_dram", [NB, P, ND * P], F16, kind="Internal").ap()
        kd_dram = nc.dram_tensor("kd_dram", [NB, P, 2 * D], F16, kind="Internal").ap()

        wsign = sb("wsign", [P, ND, DO], F16)
        alpha_b = sb("alpha_b", [P, DO])
        bias_b = sb("bias_b", [P, DO])
        kt_cur = sb("kt_cur", [P, ND, P], F16)
        kd_cur = sb("kd_cur", [P, 2, D], F16)
        xr = sb("xr", [P, RX, D])
        x1t = sb("x1t", [P, 2, 2, D], F16)
        qt = sb("qt", [P, 2, D], F16)
        xn1 = sb("xn1", [P, D])
        xn2 = sb("xn2", [P, D])
        ytmp = sb("ytmp", [P, 2, BANK])
        wstage = sb("wstage", [P, RW, D])
        kts = sb("kts", [P, 2, ND, P], F16)
        khl = x1t
        ident = sb("ident", [P, P])
        ident16 = sb("ident16", [P, P], F16)
        ones = sb("ones", [P, P])
        alpha_in = sb("alpha_in", [P, GROUP, P])
        abs_sum = sb("abs_sum", [P, NW])
        logits = sb("logits", [P, NKEY])
        ex = sb("ex", [P, NKEY])
        prob = sb("prob", [P, 2, NKEY], F16)
        pt = sb("pt", [P, P], F16)
        st1 = sb("st1", [P, NC, 6])
        st2 = sb("st2", [P, NC, 6])
        mv1 = sb("mv1", [P, 2])
        mv2 = sb("mv2", [P, 2])
        ve1 = sb("ve1", [P, 1])
        ve2 = sb("ve2", [P, 1])
        r1 = sb("r1", [P, 1])
        r2 = sb("r2", [P, 1])
        neg_half = sb("neg_half", [P, 1])
        eps = sb("eps", [P, 1])
        row_max = sb("row_max", [P, 1])
        neg_max = sb("neg_max", [P, 1])
        sum_ex = sb("sum_ex", [P, 1])
        rec_ex = sb("rec_ex", [P, 1])
        coef = sb("coef", [P, 1])
        kmax2 = sb("kmax2", [P, 2])
        kmax = sb("kmax", [P, 1])
        kmax_all = sb("kmax_all", [P, 1])
        kpow = sb("kpow", [P, 1])
        kinv = sb("kinv", [P, 1])
        kscale = sb("kscale", [P, 1])
        lscale = sb("lscale", [P, 1])
        neg_lscale = sb("neg_lscale", [P, 1])
        gates = sb("gates", [P, 2])
        tanh_g = sb("tanh_g", [P, 2])
        gx = sb("gx", [P, 1])
        gy = sb("gy", [P, 1])

        y_ps = psum("y_ps", [P, 2, BANK])
        tr_ps = psum("tr_ps", [P, 2, BANK])
        c_ps = psum("c_ps", [P, 2, BANK])
        s_ps = psum("s_ps", [P, BANK])
        w_ps = psum("w_ps", [P, BANK])
        pt_ps = s_ps[:, 2 * P:2 * P + P // 2].bitcast(F16)

        consts_in = sem("consts_in")
        bias_in = sem("bias_in")
        ctx_in = [sem(f"ctx_in{i}") for i in range(2)]
        x_in = [sem(f"x_in{s}") for s in range(RX)]
        out_done = [sem(f"out_done{s}") for s in range(RX)]
        w_in = [sem(f"w_in{s}") for s in range(RW)]
        kts_stored = sem("kts_stored")
        khl_stored = sem("khl_stored")
        kt_in = sem("kt_in")
        kd_in = sem("kd_in")
        ones_set = sem("ones_set")
        ident_zero = sem("ident_zero")
        ident_set = sem("ident_set")
        ident16_set = sem("ident16_set")
        half_set = sem("half_set")
        kmax2_set = sem("kmax2_set")
        kmax_set = sem("kmax_set")
        kmax_all_set = sem("kmax_all_set")
        kchain = sem("kchain")
        tanh_set = sem("tanh_set")
        gchain = sem("gchain")
        khl_high = sem("khl_high")
        khl_low = sem("khl_low")
        k_high = sem("k_high")
        w_tr = sem("w_tr")
        w_signed = sem("w_signed")
        w_abs = sem("w_abs")
        alpha_in_set = sem("alpha_in_set")
        alpha_tr = sem("alpha_tr")
        alpha_set = sem("alpha_set")
        stats1 = sem("stats1")
        mv1_set = sem("mv1_set")
        ve1_set = sem("ve1_set")
        r1_set = sem("r1_set")
        xn1_set = sem("xn1_set")
        tr_full = sem("tr_full")
        tr_free = sem("tr_free")
        q_high = sem("q_high")
        scores_ready = sem("scores_ready")
        logits_set = sem("logits_set")
        max_set = sem("max_set")
        neg_max_set = sem("neg_max_set")
        ex_set = sem("ex_set")
        rec_set = sem("rec_set")
        coef_set = sem("coef_set")
        prob_high = sem("prob_high")
        prob_set = sem("prob_set")
        pt_full = sem("pt_full")
        pt_set = sem("pt_set")
        c_ready = sem("c_ready")
        x1_set = sem("x1_set")
        stats2 = sem("stats2")
        mv2_set = sem("mv2_set")
        ve2_set = sem("ve2_set")
        r2_set = sem("r2_set")
        xn2_set = sem("xn2_set")
        x1b_set = sem("x1b_set")
        x1_high = sem("x1_high")
        y_ready = sem("y_ready")
        y_scaled = sem("y_scaled")
        y_added = sem("y_added")

        def chunk(n):
            return slice(n * BANK, (n + 1) * BANK)

        block = ctx.enter_context(nc.Block())

        @block.sync
        def _(sp):
            sp.dma_start(gates[:, 0:1], g_xattn.partition_broadcast(P)).then_inc(consts_in, 16)
            sp.dma_start(gates[:, 1:2], g_ffn.partition_broadcast(P)).then_inc(consts_in, 16)
            sp.dma_start(xr[:, 0, :], x_t[0]).then_inc(x_in[0], 16)
            for i in range(2):
                sp.dma_start(xr[:, 2 + i, :], ctx_t[i]).then_inc(ctx_in[i], 16)

            def load_w(w):
                if w >= RW:
                    sp.wait_ge(w_tr, NG * (w - RW + 1))
                    sp.wait_ge(w_abs, w - RW + 1)
                sp.dma_start(wstage[:, w % RW, :], w_t[w]).then_inc(w_in[w % RW], 16)

            def load_kt(batch):
                sp.dma_start(kt_cur[:, :, :].rearrange("p a b -> p (a b)"), kt_dram[batch]).then_inc(kt_in, 16)

            def load_kd(batch):
                sp.dma_start(kd_cur[:, :, :].rearrange("p a b -> p (a b)"), kd_dram[batch]).then_inc(kd_in, 16)

            load_w(0)
            sp.dma_start(xr[:, 1, :], x_t[1]).then_inc(x_in[1], 16)
            sp.dma_start(bias_b[:, :], bias.partition_broadcast(P)).then_inc(bias_in, 16)
            load_w(1)
            load_w(2)
            sp.wait_ge(kts_stored, 32)
            load_kt(0)
            sp.wait_ge(khl_stored, 16 * 8)
            load_kd(0)
            for i in range(2):
                load_w(3 + i)
                sp.wait_ge(tr_full, SEQ_KEYS + NG * (i + 1))
                sp.wait_ge(khl_low, i + 1)
                sp.dma_start(xr[:, 2 + i, :], x_t[2 + i]).then_inc(x_in[2 + i], 16)
            for w in range(5, NW):
                load_w(w)

            def store(u, r):
                sp.wait_ge(y_added, 7 if isinstance(u, int) and u == 0 else u * NC + NC)
                sp.dma_start(out_t[u], xr[:, r, :]).then_inc(out_done[r], 16)

            def reload(u, r, times):
                sp.wait_ge(out_done[r], times * 16)
                sp.dma_start(xr[:, r, :], x_t[u + RX]).then_inc(x_in[r], 16)

            store(0, 0)
            reload(0, 0, 1)
            with sp.Fori(0, LOOPS - 1) as i:
                for j in range(STEPS):
                    u, r = i * STEPS + (1 + j), (1 + j) % RX
                    store(u, r)
                    reload(u, r, i + (1 if j < 3 else 2))
                batch = (i + 2) // 2
                sp.wait_ge(scores_ready, i * STEPS + 2 * STEPS)
                load_kt(batch)
                sp.wait_ge(c_ready, i * STEPS * NC + 2 * STEPS * NC)
                load_kd(batch)
            for u in range(NT - RX - 3, NT - RX):
                store(u, u % RX)
                reload(u, u % RX, u // RX + 1)
            for r in range(RX):
                store(NT - RX + r, r)
            for r in range(RX):
                sp.wait_ge(out_done[r], 16 * (NT // RX))

        @block.gpsimd
        def _(pool):
            nc.gpsimd.memset(ident[:, :], 0.0).then_inc(ident_zero, 1)
            pool.wait_ge(ident_zero, 1)
            nc.gpsimd.affine_select(out=ident[:, :], in_=ident[:, :], compare_op=ALU.not_equal, fill=1.0, base=0,
                                    pattern=[[-1, P]], channel_multiplier=1).then_inc(ident_set, 1)
            nc.gpsimd.memset(neg_half[:, :], -0.5).then_inc(half_set, 1)
            nc.gpsimd.memset(eps[:, :], EPS).then_inc(half_set, 1)
            pool.wait_ge(half_set, 2)

            def rstd(u, mv, ve, r, mv_set, ve_set, r_set):
                pool.wait_ge(mv_set, u + 1)
                nc.gpsimd.tensor_tensor(ve[:, :], mv[:, 1:2], eps[:, :], ALU.add).then_inc(ve_set, 1)
                pool.wait_ge(ve_set, u + 1)
                nc.gpsimd.tensor_tensor(r[:, :], ve[:, :], neg_half[:, :], ALU.pow).then_inc(r_set, 1)

            def rstd1(u):
                rstd(u, mv1, ve1, r1, mv1_set, ve1_set, r1_set)

            def rstd2(u):
                rstd(u, mv2, ve2, r2, mv2_set, ve2_set, r2_set)

            def add_bias(u, r):
                pool.wait_ge(xn2_set, u + 1)
                nc.gpsimd.tensor_tensor(xr[:, r, :], xr[:, r, :], bias_b[:, :], ALU.add).then_inc(x1b_set, 1)

            pool.wait_ge(kmax_set, 1)
            nc.gpsimd.partition_all_reduce(kmax_all[:, :], kmax[:, :], P, bass.bass_isa.ReduceOp.max).then_inc(kmax_all_set, 1)
            rstd1(0)
            for i in range(2):
                pool.wait_ge(khl_low, i + 1)
                for b in range(2):
                    for c in range(2):
                        pool.dma_start(kd_dram[2 * i + b, NKEY * c:NKEY * (c + 1), :],
                                       khl[NKEY * b:NKEY * (b + 1), i, :, :].rearrange("p a b -> p (a b)")).then_inc(khl_stored, 16)
                pool.wait_ge(tr_free, SEQ_KEYS + NG * (i + 1))
                pool.dma_start(kt_dram[2 * i:2 * i + 2].rearrange("b p n -> p b n"),
                               kts[:, :, :, :].rearrange("p b a k -> p b (a k)")).then_inc(kts_stored, 16)
            rstd1(1)
            pool.wait_ge(gchain, 3)
            for u in range(2):
                rstd2(u)
                add_bias(u, u)
            for u in range(2, 4):
                rstd1(u)
                rstd2(u)
                add_bias(u, u)
            with pool.Fori(0, LOOPS) as i:
                for j in range(STEPS):
                    u = i * STEPS + (STEPS + j)
                    rstd1(u)
                    rstd2(u)
                    add_bias(u, j)

        @block.scalar
        def _(act):
            def high_group(dst, g, seq, done):
                act.wait_ge(tr_full, seq + g + 1)
                nc.scalar.activation(dst[:, chunk(g)], tr_ps[:, g % 2, :], ACT.Copy, scale=LN_SCALE).then_inc(done, 1)

            def high_x(u, g):
                if g == 0 and not (isinstance(u, int) and u == 0):
                    act.wait_ge(scores_ready, u)
                high_group(qt[:, 0, :], g, seq_xT(u), q_high)

            def high_x1(u, g, slot):
                if g == 0:
                    if not isinstance(u, int) or u >= 4:
                        act.wait_ge(y_ready, u * NC - NC)
                    elif u >= 2:
                        act.wait_ge(y_ready, 7 + u - 2)
                high_group(x1t[:, slot, 0, :], g, seq_x1T(u), x1_high)

            def exp(u):
                act.wait_ge(neg_max_set, u + 1)
                nc.scalar.activation(ex[:, :], logits[:, :], ACT.Exp, bias=neg_max[:, :], scale=lscale[:, :],
                                     accum_out=sum_ex[:, :]).then_inc(ex_set, 1)

            def copy_pt(u):
                act.wait_ge(pt_full, u + 1)
                nc.scalar.copy(pt[:, :], pt_ps).then_inc(pt_set, 1)

            def sign_group(m):
                w, g = m // NG, m % NG
                act.wait_ge(w_tr, m + 1)
                src = y_ps[:, m % 2, :] if m < 16 else w_ps[:, :]
                nc.scalar.activation(wsign[:, GROUP * g:GROUP * (g + 1), P * w:P * (w + 1)],
                                     src.rearrange("p (a b) -> p a b", a=GROUP), ACT.Sign).then_inc(w_signed, 1)

            def key_high(i, g):
                act.wait_ge(tr_full, SEQ_KEYS + NG * i + g + 1)
                if i == 1 and g == 0:
                    act.wait_ge(kts_stored, 16)
                src = tr_ps[:, g % 2, :].rearrange("p (a b k) -> p b a k", a=GROUP, b=2)
                for b in range(2):
                    last = nc.scalar.activation(kts[:, b, GROUP * g:GROUP * (g + 1), 0:NKEY], src[:, b], ACT.Copy,
                                                scale=kscale[:, :])
                last.then_inc(k_high, 1)

            act.wait_ge(consts_in, 32)
            nc.scalar.activation(tanh_g[:, :], gates[:, :], ACT.Tanh).then_inc(tanh_set, 1)
            for g in range(NG):
                high_x(0, g)
            act.wait_ge(kchain, 4)
            for i in range(2):
                act.wait_ge(ctx_in[i], 16)
                nc.scalar.activation(khl[:, i, 0, :], xr[:, 2 + i, :], ACT.Copy, scale=kscale[:, :]).then_inc(khl_high, 1)
                for g in range(NG):
                    key_high(i, g)
            for m in range(8):
                sign_group(m)
            exp(0)
            for g in range(NG):
                high_x(1, g)
            for m in range(8, 12):
                sign_group(m)
            copy_pt(0)
            exp(1)
            for m in range(12, 16):
                sign_group(m)
            act.wait_ge(c_ready, NC)
            copy_pt(1)
            for g in range(NG):
                high_x1(0, g, 0)
            for g in range(NG):
                high_x1(1, g, 1)

            for k in range(PAIR_BLOCKS):
                if k < 24:
                    sign_group(16 + 2 * k)
                    sign_group(17 + 2 * k)
                if k in PAIR_XT:
                    high_x(*PAIR_XT[k])
                if k in PAIR_SCORES:
                    exp(PAIR_SCORES[k])
                if k in PAIR_PT:
                    act.wait_ge(c_ready, NC * PAIR_PT[k])
                    copy_pt(PAIR_PT[k])
                for g in PAIR_X1T.get(k, []):
                    high_x1(2, g, 0)

            def step(t, r, attention=True):
                for g in range(NG):
                    high_x1(t + 1, g, (r + 1) % 2)
                if attention:
                    for g in range(NG):
                        high_x(t + 2, g)
                    exp(t + 2)
                    act.wait_ge(c_ready, t * NC + 2 * NC)
                    copy_pt(t + 2)

            with act.Fori(0, LOOPS) as i:
                for j in range(STEPS):
                    step(i * STEPS + (2 + j), (2 + j) % 4)
            step(NT - 2, (NT - 2) % 4, attention=False)

        @block.vector
        def _(dve):
            def norm_stats1(u, r, n):
                if n == 0:
                    dve.wait_ge(x_in[r], 16 if isinstance(u, int) and u < 4 else load_count(u, r))
                nc.vector.bn_stats(st1[:, n, :], xr[:, r, chunk(n)]).then_inc(stats1, 1)

            def load_count(u, r):
                return (u - r) * (16 // RX) + 16

            def stats1_done(u):
                dve.wait_ge(stats1, u * NC + NC)

            def stats2_done(u):
                dve.wait_ge(stats2, u * NC + NC)

            def norm_mean1(u):
                nc.vector.bn_aggr(mv1[:, :], st1[:, :, :].rearrange("p a b -> p (a b)")).then_inc(mv1_set, 1)

            def normalise1(u, r):
                dve.wait_ge(r1_set, u + 1)
                nc.vector.tensor_scalar(xn1[:, :], xr[:, r, :], mv1[:, 0:1], r1[:, 0:1], ALU.subtract,
                                        ALU.mult).then_inc(xn1_set, 1)

            def norm_mean2(u):
                nc.vector.bn_aggr(mv2[:, :], st2[:, :, :].rearrange("p a b -> p (a b)")).then_inc(mv2_set, 1)

            def normalise2(u, r):
                dve.wait_ge(r2_set, u + 1)
                nc.vector.tensor_scalar(xn2[:, :], xr[:, r, :], mv2[:, 0:1], r2[:, 0:1], ALU.subtract,
                                        ALU.mult).then_inc(xn2_set, 1)

            def low_x(u, g):
                dve.wait_ge(q_high, u * NG + (g + 1))
                nc.vector.scalar_tensor_tensor(out=qt[:, 1, chunk(g)], in0=tr_ps[:, g % 2, :], scalar=LN_SCALE,
                                               in1=qt[:, 0, chunk(g)], op0=ALU.mult, op1=ALU.subtract).then_inc(tr_free, 1)

            def low_x1(u, g, slot):
                dve.wait_ge(x1_high, u * NG + (g + 1))
                nc.vector.scalar_tensor_tensor(out=x1t[:, slot, 1, chunk(g)], in0=tr_ps[:, g % 2, :], scalar=LN_SCALE,
                                               in1=x1t[:, slot, 0, chunk(g)], op0=ALU.mult,
                                               op1=ALU.subtract).then_inc(tr_free, 1)

            def max_logits(u):
                dve.wait_ge(scores_ready, u + 1)
                nc.vector.tensor_reduce(logits[:, :], s_ps[:, 0:P].rearrange("p (h k) -> p k h", h=2), X,
                                        ALU.add).then_inc(logits_set, 1)
                dve.wait_ge(logits_set, u + 1)
                nc.vector.tensor_reduce(row_max[:, :], logits[:, :], X, ALU.max).then_inc(max_set, 1)
                dve.wait_ge(max_set, u + 1)
                nc.vector.tensor_scalar(neg_max[:, :], row_max[:, :], neg_lscale[:, 0:1], None,
                                        ALU.mult).then_inc(neg_max_set, 1)

            def split_probs(u):
                dve.wait_ge(ex_set, u + 1)
                nc.vector.tensor_scalar(prob[:, 0, :], ex[:, :], PROB_SCALE, None, ALU.mult).then_inc(prob_high, 1)
                nc.vector.reciprocal(rec_ex[:, :], sum_ex[:, :]).then_inc(rec_set, 1)
                dve.wait_ge(prob_high, u + 1)
                nc.vector.scalar_tensor_tensor(out=prob[:, 1, :], in0=ex[:, :], scalar=PROB_SCALE, in1=prob[:, 0, :],
                                               op0=ALU.mult, op1=ALU.subtract).then_inc(prob_set, 1)
                dve.wait_ge(rec_set, u + 1)
                nc.vector.tensor_scalar(coef[:, :], rec_ex[:, :], gx[:, 0:1], None, ALU.mult).then_inc(coef_set, 1)

            def add_attention(u, r, n):
                dve.wait_ge(c_ready, u * NC + (n + 1))
                if n == 0:
                    dve.wait_ge(coef_set, u + 1)
                nc.vector.scalar_tensor_tensor(out=xr[:, r, chunk(n)], in0=c_ps[:, n % 2, :], scalar=coef[:, 0:1],
                                               in1=xr[:, r, chunk(n)], op0=ALU.mult, op1=ALU.add).then_inc(x1_set, 1)

            def norm_stats2(u, r, n):
                dve.wait_ge(x1_set, u * NC + (n + 1))
                nc.vector.bn_stats(st2[:, n, :], xr[:, r, chunk(n)]).then_inc(stats2, 1)

            def scale_y(t, n, r):
                k = seq_y(t, n)
                bank = (t if isinstance(t, int) and t < 2 else n) % 2
                dve.wait_ge(y_ready, k + 1)
                nc.vector.tensor_tensor(ytmp[:, bank, :], y_ps[:, bank, :], alpha_b[:, chunk(n)],
                                        ALU.mult).then_inc(y_scaled, 1)

            def add_y(t, n, r):
                k = seq_y(t, n)
                bank = (t if isinstance(t, int) and t < 2 else n) % 2
                dve.wait_ge(y_scaled, k + 1)
                dve.wait_ge(x1b_set, t + 1)
                nc.vector.tensor_tensor(xr[:, r, chunk(n)], ytmp[:, bank, :], xr[:, r, chunk(n)],
                                        ALU.add).then_inc(y_added, 1)

            def finish_y(t, n, r):
                scale_y(t, n, r)
                add_y(t, n, r)

            def sum_abs(w):
                dve.wait_ge(w_in[w % RW], 16 * (w // RW + 1))
                nc.vector.tensor_reduce(abs_sum[:, w:w + 1], wstage[:, w % RW, :], X, ALU.add,
                                        apply_absolute_value=True).then_inc(w_abs, 1)

            def spread_alpha(w):
                dve.wait_ge(w_abs, w + 1)
                if w >= GROUP:
                    dve.wait_ge(alpha_tr, w // GROUP)
                nc.vector.tensor_scalar(alpha_in[:, w % GROUP, :], ones[:, :], abs_sum[:, w:w + 1], None,
                                        ALU.mult).then_inc(alpha_in_set, 1)

            def take_alpha(n):
                dve.wait_ge(alpha_tr, n + 1)
                nc.vector.tensor_scalar(alpha_b[:, chunk(n)], w_ps[:, :], gy[:, 0:1], None, ALU.mult).then_inc(alpha_set, 1)

            def key_low(i, g):
                dve.wait_ge(k_high, NG * i + g + 1)
                src = tr_ps[:, g % 2, :].rearrange("p (a b k) -> p b a k", a=GROUP, b=2)
                for b in range(2):
                    dst = kts[:, b, GROUP * g:GROUP * (g + 1), :]
                    last = nc.vector.scalar_tensor_tensor(out=dst[:, :, NKEY:], in0=src[:, b], scalar=kscale[:, 0:1],
                                                          in1=dst[:, :, 0:NKEY], op0=ALU.mult, op1=ALU.subtract)
                last.then_inc(tr_free, 1)

            nc.vector.memset(ones[:, :], 1.0).then_inc(ones_set, 1)
            for n in range(NC):
                norm_stats1(0, 0, n)
            stats1_done(0)
            norm_mean1(0)
            for i in range(2):
                dve.wait_ge(ctx_in[i], 16)
                nc.vector.tensor_reduce(kmax2[:, i:i + 1], xr[:, 2 + i, :], X, ALU.max,
                                        apply_absolute_value=True).then_inc(kmax2_set, 1)
            dve.wait_ge(kmax2_set, 2)
            nc.vector.tensor_reduce(kmax[:, :], kmax2[:, :], X, ALU.max).then_inc(kmax_set, 1)
            normalise1(0, 0)
            dve.wait_ge(kmax_all_set, 1)
            nc.vector.tensor_scalar(kpow[:, :].bitcast(I32), kmax_all[:, :].bitcast(I32), 0x7F800000, None,
                                    ALU.bitwise_and).then_inc(kchain, 1)
            dve.wait_ge(kchain, 1)
            nc.vector.tensor_scalar(kinv[:, :], kpow[:, :], 2.0 ** -90, 1.0 / KEY_TOP, ALU.max, ALU.mult).then_inc(kchain, 1)
            dve.wait_ge(kchain, 2)
            nc.vector.reciprocal(kscale[:, :], kinv[:, :]).then_inc(kchain, 1)
            dve.wait_ge(kchain, 3)
            nc.vector.tensor_scalar(lscale[:, :], kinv[:, :], 1.0 / LN_SCALE, None, ALU.mult).then_inc(kchain, 1)
            nc.vector.tensor_scalar(neg_lscale[:, :], kinv[:, :], -1.0 / LN_SCALE, None, ALU.mult).then_inc(kchain, 1)
            dve.wait_ge(tanh_set, 1)
            nc.vector.tensor_scalar(gx[:, :], tanh_g[:, 0:1], kinv[:, 0:1], 1.0 / PROB_SCALE, ALU.mult,
                                    ALU.mult).then_inc(gchain, 1)
            nc.vector.tensor_scalar(gy[:, :], tanh_g[:, 1:2], 1.0 / (D * LN_SCALE), None, ALU.mult).then_inc(gchain, 1)
            dve.wait_ge(kchain, 5)
            dve.wait_ge(gchain, 2)
            for g in range(NG):
                low_x(0, g)
            for i in range(2):
                dve.wait_ge(khl_high, i + 1)
                nc.vector.scalar_tensor_tensor(out=khl[:, i, 1, :], in0=xr[:, 2 + i, :], scalar=kscale[:, 0:1],
                                               in1=khl[:, i, 0, :], op0=ALU.mult, op1=ALU.subtract).then_inc(khl_low, 1)
                for g in range(NG):
                    key_low(i, g)
            dve.wait_ge(ident_set, 1)
            nc.vector.tensor_copy(ident16[:, :], ident[:, :]).then_inc(ident16_set, 1)
            dve.wait_ge(ones_set, 1)
            sum_abs(0)
            for n in range(NC):
                norm_stats1(1, 1, n)
            stats1_done(1)
            norm_mean1(1)
            spread_alpha(0)
            sum_abs(1)
            normalise1(1, 1)
            spread_alpha(1)
            dve.wait_ge(bias_in, 16)
            nc.vector.tensor_scalar(bias_b[:, :], bias_b[:, :], tanh_g[:, 1:2], None, ALU.mult).then_inc(gchain, 1)
            max_logits(0)
            for g in range(NG):
                low_x(1, g)
            split_probs(0)
            sum_abs(2)
            for n in range(NC):
                add_attention(0, 0, n)
            spread_alpha(2)
            max_logits(1)
            for n in range(NC):
                norm_stats2(0, 0, n)
            stats2_done(0)
            norm_mean2(0)
            split_probs(1)
            sum_abs(3)
            normalise2(0, 0)
            spread_alpha(3)
            for n in range(NC):
                low_x1(0, n, 0)
            for n in range(NC):
                add_attention(1, 1, n)
            take_alpha(0)
            for n in range(NC):
                norm_stats2(1, 1, n)
            stats2_done(1)
            norm_mean2(1)
            normalise2(1, 1)
            for n in range(NC):
                low_x1(1, n, 1)

            for k in range(PAIR_BLOCKS):
                if k < 24 and k % 2 == 0:
                    w = GROUP + k // 2
                    sum_abs(w)
                    spread_alpha(w)
                if k in (2, 14):
                    u = 2 if k == 2 else 3
                    for n in range(NC):
                        norm_stats1(u, u, n)
                    stats1_done(u)
                    norm_mean1(u)
                if k == 15:
                    normalise2(2, 2)
                if k in (3, 15):
                    u = 2 if k == 3 else 3
                    normalise1(u, u)
                if k in PAIR_XT:
                    low_x(*PAIR_XT[k])
                if k in PAIR_SCORES:
                    max_logits(PAIR_SCORES[k])
                    split_probs(PAIR_SCORES[k])
                if k in PAIR_C:
                    u, n = PAIR_C[k]
                    add_attention(u, u, n)
                    norm_stats2(u, u, n)
                    if n == NC - 1:
                        stats2_done(u)
                        norm_mean2(u)
                if k in PAIR_ALPHA:
                    take_alpha(PAIR_ALPHA[k])
                if k % 4 == 3:
                    if k == 3:
                        dve.wait_ge(alpha_set, 1)
                    if k in (11, 19, 27):
                        dve.wait_ge(alpha_set, k // 8 + 1)
                    finish_y(k // 4 % 2, k // 8, k // 4 % 2)
                for g in PAIR_X1T.get(k, []):
                    low_x1(2, g, 0)
            normalise2(3, 3)

            def step(t, r, x1=True, attention=True):
                a, ra = t + 2, (r + 2) % RX
                slot = (r + 1) % 2
                if x1:
                    low_x1(t + 1, 0, slot)
                if attention:
                    norm_stats1(a, ra, 0)
                    norm_stats1(a, ra, 1)
                if x1:
                    low_x1(t + 1, 1, slot)
                if attention:
                    norm_stats1(a, ra, 2)
                    norm_stats1(a, ra, 3)
                if attention:
                    stats1_done(a)
                if x1:
                    low_x1(t + 1, 2, slot)
                if attention:
                    norm_mean1(a)
                if x1:
                    low_x1(t + 1, 3, slot)
                if attention:
                    normalise1(a, ra)
                finish_y(t, 0, r)
                if attention:
                    for g in range(3):
                        low_x(a, g)
                finish_y(t, 1, r)
                if attention:
                    low_x(a, 3)
                    max_logits(a)
                    split_probs(a)
                    add_attention(a, ra, 0)
                if attention:
                    norm_stats2(a, ra, 0)
                    for n in range(1, NC):
                        add_attention(a, ra, n)
                        norm_stats2(a, ra, n)
                    stats2_done(a)
                finish_y(t, 2, r)
                if attention:
                    norm_mean2(a)
                    normalise2(a, ra)
                finish_y(t, 3, r)

            with dve.Fori(0, LOOPS) as i:
                for j in range(STEPS):
                    step(i * STEPS + (2 + j), (2 + j) % RX)
            step(NT - 2, (NT - 2) % RX, attention=False)
            step(NT - 1, (NT - 1) % RX, x1=False, attention=False)

        @block.tensor
        def _(pe):
            def transposes(src, dst, done):
                for b in range(GROUP):
                    last = nc.tensor.transpose(dst[:, P * b:P * (b + 1)], src[:, P * b:P * (b + 1)], ident[:, :])
                last.then_inc(done, 1)

            def through_bank(src, seq, g):
                if not (isinstance(seq, int) and seq + g < 2):
                    pe.wait_ge(tr_free, seq + (g - 1))
                transposes(src, tr_ps[:, g % 2, :], tr_full)

            def transpose_x(u, g):
                if g == 0:
                    pe.wait_ge(xn1_set, u + 1)
                through_bank(xn1[:, chunk(g)], seq_xT(u), g)

            def transpose_x1(u, g):
                if g == 0:
                    pe.wait_ge(xn2_set, u + 1)
                through_bank(xn2[:, chunk(g)], seq_x1T(u), g)

            def transpose_keys(i, g):
                if g == 0:
                    pe.wait_ge(ctx_in[i], 16)
                through_bank(xr[:, 2 + i, chunk(g)], SEQ_KEYS + NG * i, g)

            def transpose_w(m):
                w, g = m // NG, m % NG
                if g == 0:
                    pe.wait_ge(w_in[w % RW], 16 * (w // RW + 1))
                if 2 <= m < 16:
                    pe.wait_ge(w_signed, m - 1)
                elif m > 16:
                    pe.wait_ge(w_signed, m)
                if m >= 16 and m % 16 == 0:
                    pe.wait_ge(alpha_set, m // 16)
                transposes(wstage[:, w % RW, chunk(g)], y_ps[:, m % 2, :] if m < 16 else w_ps[:, :], w_tr)

            def transpose_alpha(n):
                pe.wait_ge(alpha_in_set, GROUP * (n + 1))
                if n > 0:
                    pe.wait_ge(w_signed, 16 * (n + 1))
                transposes(alpha_in[:, :, :].rearrange("p a b -> p (a b)"), w_ps[:, :], alpha_tr)

            def scores(u):
                pe.wait_ge(tr_free, seq_xT(u) + NG)
                for k in range(ND):
                    for part in range(2):
                        last = nc.tensor.matmul(s_ps[:, 0:P], qt[:, part, P * k:P * (k + 1)], kt_cur[:, k, :],
                                                start=(k == 0 and part == 0), stop=(k == ND - 1 and part == 1))
                last.then_inc(scores_ready, 1)

            def transpose_probs(u):
                pe.wait_ge(prob_set, u + 1)
                nc.tensor.transpose(pt_ps, prob[:, :, :].rearrange("p a b -> p (a b)"), ident16[:, :]).then_inc(pt_full, 1)

            def attend(u, n):
                if n == 0:
                    pe.wait_ge(pt_set, u + 1)
                if not (isinstance(u, int) and u == 0 and n < 2):
                    pe.wait_ge(x1_set, u * NC + (n - 1))
                for part in range(2):
                    last = nc.tensor.matmul(c_ps[:, n % 2, :], pt[:, :], kd_cur[:, part, chunk(n)],
                                            start=(part == 0), stop=(part == 1))
                last.then_inc(c_ready, 1)

            def ffn_block(bank, slot, n, q):
                for k in range(4 * q, 4 * q + 4):
                    for part in range(2):
                        last = nc.tensor.matmul(y_ps[:, bank, :], x1t[:, slot, part, P * k:P * (k + 1)],
                                                wsign[:, k, chunk(n)], start=(k == 0 and part == 0),
                                                stop=(k == ND - 1 and part == 1))
                if q == 3:
                    last.then_inc(y_ready, 1)

            pe.wait_ge(ident_set, 1)
            for g in range(NG):
                transpose_x(0, g)
            for i in range(2):
                for g in range(NG):
                    transpose_keys(i, g)
            for m in range(8):
                transpose_w(m)
            pe.wait_ge(kt_in, 16)
            scores(0)
            for g in range(NG):
                transpose_x(1, g)
            for m in range(8, 12):
                transpose_w(m)
            pe.wait_ge(ident16_set, 1)
            transpose_probs(0)
            pe.wait_ge(kd_in, 16)
            for n in range(NC):
                attend(0, n)
            scores(1)
            for m in range(12, 16):
                transpose_w(m)
            transpose_probs(1)
            for g in range(NG):
                transpose_x1(0, g)
            for n in range(NC):
                attend(1, n)
            transpose_alpha(0)
            for g in range(NG):
                transpose_x1(1, g)

            for k in range(PAIR_BLOCKS):
                n, tile, q = k // 8, k // 4 % 2, k % 4
                if q == 0:
                    if tile == 0:
                        pe.wait_ge(w_signed, 16 * (n + 1))
                    if n == 0:
                        pe.wait_ge(tr_free, seq_x1T(tile) + NG)
                    if n > 0:
                        pe.wait_ge(y_scaled, 2 * n + tile - 1)
                ffn_block(tile, tile, n, q)
                if k < 24:
                    transpose_w(16 + 2 * k)
                    transpose_w(17 + 2 * k)
                if k in PAIR_ALPHA:
                    transpose_alpha(PAIR_ALPHA[k])
                if k in PAIR_XT:
                    transpose_x(*PAIR_XT[k])
                if k in PAIR_SCORES:
                    scores(PAIR_SCORES[k])
                if k in PAIR_PT:
                    transpose_probs(PAIR_PT[k])
                if k in PAIR_C:
                    attend(*PAIR_C[k])
                for g in PAIR_X1T.get(k, []):
                    transpose_x1(2, g)

            def step(t, r, x1=True, attention=True, keys=None):
                pe.wait_ge(tr_free, seq_x1T(t) + NG)
                for k in range(BLOCKS):
                    n, q = k // 4, k % 4
                    if q == 0:
                        pe.wait_ge(y_scaled, t * NC + (n - 1))
                    ffn_block(n % 2, r % 2, n, q)
                    if x1:
                        for g in X1T_AT.get(k, []):
                            transpose_x1(t + 1, g)
                    if attention:
                        if k in XT_AT:
                            transpose_x(t + 2, XT_AT[k])
                        if k == SCORES_AT:
                            if keys is not None:
                                pe.wait_ge(kt_in, keys)
                            scores(t + 2)
                        if k == PT_AT:
                            transpose_probs(t + 2)
                        if k in C_AT:
                            if C_AT[k] == 0 and keys is not None:
                                pe.wait_ge(kd_in, keys)
                            attend(t + 2, C_AT[k])

            with pe.Fori(0, LOOPS) as i:
                for j in range(STEPS):
                    step(i * STEPS + (2 + j), (2 + j) % RX, keys=i * 16 + 16 if j == 0 else None)
            step(NT - 2, (NT - 2) % RX, attention=False)
            step(NT - 1, (NT - 1) % RX, x1=False, attention=False)


_INS = ['x', 'ctx_4096', 'g_xattn', 'g_ffn', 'L0_ffn_weight_real', 'L0_ffn_bias']
_OUTS = [((4, 1024, 2048), 'float32')]


def kernel(**inputs):
    import numpy as _np
    import concourse.bacc as _bacc
    from concourse import mybir as _mybir
    from concourse.bass_utils import run_bass_kernel_spmd as _run

    nc = _bacc.Bacc("TRN2", target_bir_lowering=False, num_devices=1)
    arrays, args = {}, []
    for name in _INS:
        a = _np.ascontiguousarray(inputs[name])
        arrays[f"in_{name}_dram"] = a
        args.append(nc.dram_tensor(f"in_{name}_dram", a.shape, _mybir.dt.from_np(a.dtype), kind="ExternalInput").ap())
    for i, (shape, dtype) in enumerate(_OUTS):
        dt = _mybir.dt.from_np(_np.dtype(dtype))
        args.append(nc.dram_tensor(f"out_{i}_dram", shape, dt, kind="ExternalOutput").ap())
    flamingo_gated_kernel(nc, *args)
    r = _run(nc, [arrays], core_ids=[0])
    got = tuple(r.results[0][f"out_{i}_dram"] for i in range(len(_OUTS)))
    return got[0]
```

```python
import concourse.bass as bass
from concourse import mybir
from contextlib import ExitStack

P = 128
BANK = 512
GROUP = BANK // P
LN_SCALE = 2.0 ** 10
PROB_SCALE = 2.0 ** 14
KEY_TOP = 2.0 ** 14
EPS = 1e-5


def flamingo_gated_kernel(
    nc: bass.Bass,
    x: bass.AP,
    ctx_keys: bass.AP,
    g_xattn: bass.AP,
    g_ffn: bass.AP,
    weight: bass.AP,
    bias: bass.AP,
    out: bass.AP,
):
    F32, F16, I32 = mybir.dt.float32, mybir.dt.float16, mybir.dt.int32
    ALU = mybir.AluOpType
    ACT = mybir.ActivationFunctionType
    X = mybir.AxisListType.X

    NB, S, D = x.shape
    NKEY = ctx_keys.shape[1]
    DO = weight.shape[0]
    NT = NB * S // P
    ND = D // P
    NC = D // BANK
    NG = ND // GROUP
    Q = P // 4
    NW = DO // P
    TILES_PER_BATCH = S // P
    RX, RW, RB = 4, 4, 3
    STEPS = 4
    FIRST = 3
    LOOPS = (NT - 5 - FIRST) // STEPS
    BLOCKS = 16
    assert NKEY * 2 == P and D == DO and NC == 4 and NG == 4 and NB == 4
    assert TILES_PER_BATCH == 2 * STEPS and NT == FIRST + STEPS * LOOPS + 5

    x_t = x.rearrange("b (t p) d -> (b t) p d", p=P)
    x_q = x.rearrange("b (t i c) (a n) -> (b t) a i c n", c=4, i=Q, a=4)
    out_t = out.rearrange("b (t p) d -> (b t) p d", p=P)
    ctx_t = ctx_keys.rearrange("(i b) k (a h n) -> i h (b k) a n", b=2, a=4, h=2)
    w_t = weight.rearrange("(t p) (a h n) -> t h p a n", p=P, a=4, h=2)

    SCORES_AT, PT_AT, C_AT, SPREAD_AT = 2, 4, {6: 0, 7: 1, 8: 2, 9: 3}, 8
    LATE_SCORES_AT, LATE_PT_AT, LATE_C_AT, LATE_SPREAD_AT = 9, 11, {12: 0, 13: 1, 14: 2, 15: 3}, 14
    LATE_FIRST_SPREAD_AT = 4
    PAIR_BLOCKS = 32
    PAIR_SPREAD = {3: 2, 15: 3}
    PAIR_SCORES = {8: 2, 20: 3}
    PAIR_PT = {10: 2, 22: 3}
    PAIR_C = {11: (2, 0), 12: (2, 1), 13: (2, 2), 14: (2, 3), 23: (3, 0), 24: (3, 1), 25: (3, 2), 26: (3, 3)}
    PAIR_ALPHA = {7: 1, 15: 2, 23: 3}
    CHUNK_GROUPS = NG * GROUP

    setup_order = [("keys", n) for n in range(2 * NG)] + [("w", m) for m in range(CHUNK_GROUPS)] + [("alpha", 0)]
    for n in range(1, NC):
        setup_order += [("w", m) for m in range(CHUNK_GROUPS * n, CHUNK_GROUPS * (n + 1))] + [("alpha", n)]

    def seq_y(t, n):
        return 2 * n + t if isinstance(t, int) and t < 2 else t * 4 + n

    with ExitStack() as ctx:
        def sb(name, shape, dt=F32):
            return ctx.enter_context(nc.sbuf_tensor(name, shape, dt))

        def psum(name, shape):
            return ctx.enter_context(nc.psum_tensor(name, shape, F32))

        def sem(name):
            return ctx.enter_context(nc.semaphore(name))

        kt_dram = nc.dram_tensor("kt_dram", [NB, P, ND * P], F16, kind="Internal").ap()
        kd_dram = nc.dram_tensor("kd_dram", [NB, P, 2 * D], F16, kind="Internal").ap()

        wsign = sb("wsign", [P, ND, DO], F16)
        alpha_b = sb("alpha_b", [P, DO])
        bias_b = sb("bias_b", [P, DO])
        kt_cur = sb("kt_cur", [P, ND, P], F16)
        kd_cur = sb("kd_cur", [P, 2, D], F16)
        xr = sb("xr", [P, RX, D])
        x1t = sb("x1t", [P, 2, 2, D], F16)
        qt = sb("qt", [P, 2, D], F16)
        xs1 = sb("xs1", [P, D])
        xn1 = sb("xn1", [P, D])
        xn2 = sb("xn2", [P, D])
        xs2 = sb("xs2", [P, D])
        factors = sb("factors", [P, 2, 4])
        spread = sb("spread", [P, 2, 4])
        same_i = sb("same_i", [P, P])
        own_c = sb("own_c", [P, 4])
        ytmp = sb("ytmp", [P, 2, BANK])
        wstage = sb("wstage", [P, RW, D // 2])
        kts = [b[:, :].bitcast(F16).rearrange("p (b a k) -> p b a k", b=2, a=ND) for b in (xs2, xn2)]
        khl = x1t
        ident = sb("ident", [P, P])
        ident16 = sb("ident16", [P, P], F16)
        ones = sb("ones", [P, P])
        alpha_in = sb("alpha_in", [P, GROUP, P])
        abs_sum = sb("abs_sum", [P, 2 * NW])
        logits = sb("logits", [P, NKEY])
        ex = sb("ex", [P, NKEY])
        prob = sb("prob", [P, 2, NKEY], F16)
        pt = sb("pt", [P, P], F16)
        st1 = sb("st1", [P, NC, 6])
        st2 = sb("st2", [P, NC, 6])
        mv1 = sb("mv1", [P, 2])
        mv2 = sb("mv2", [P, 2])
        ve1 = sb("ve1", [P, 1])
        ve2 = sb("ve2", [P, 1])
        r1 = sb("r1", [P, 1])
        r2 = sb("r2", [P, 1])
        mr1 = sb("mr1", [P, 1])
        mr2 = sb("mr2", [P, 1])
        nm1 = sb("nm1", [P, 1])
        nm2 = sb("nm2", [P, 1])
        neg_half = sb("neg_half", [P, 1])
        eps = sb("eps", [P, 1])
        zero = sb("zero", [P, 1])
        row_max = sb("row_max", [P, 1])
        neg_max = sb("neg_max", [P, 1])
        sum_ex = sb("sum_ex", [P, 1])
        rec_ex = sb("rec_ex", [P, 1])
        coef = sb("coef", [P, 1])
        kmax2 = sb("kmax2", [P, 2])
        kmax = sb("kmax", [P, 1])
        kmax_all = sb("kmax_all", [P, 1])
        kpow = sb("kpow", [P, 1])
        kinv = sb("kinv", [P, 1])
        kscale = sb("kscale", [P, 1])
        lscale = sb("lscale", [P, 1])
        neg_lscale = sb("neg_lscale", [P, 1])
        gates = sb("gates", [P, 2])
        tanh_g = sb("tanh_g", [P, 2])
        gx = sb("gx", [P, 1])
        gy = sb("gy", [P, 1])

        y_ps = psum("y_ps", [P, 2, BANK])
        c_ps = psum("c_ps", [P, 2, BANK])
        s_ps = psum("s_ps", [P, BANK])
        setup_ps = psum("setup_ps", [P, RB, BANK])
        pt_ps = s_ps[:, 2 * P:2 * P + P // 2].bitcast(F16)

        consts_in = sem("consts_in")
        bias_in = sem("bias_in")
        ctx_in = [sem(f"ctx_in{i}") for i in range(2)]
        x_in = [sem(f"x_in{s}") for s in range(RX)]
        out_done = [sem(f"out_done{s}") for s in range(RX)]
        w_in = [sem(f"w_in{s}") for s in range(RW)]
        kts_stored = [sem(f"kts_stored{i}") for i in range(2)]
        khl_stored = [sem(f"khl_stored{i}") for i in range(2)]
        kt_in = sem("kt_in")
        kd_in = sem("kd_in")
        xs1_in = sem("xs1_in")
        moved2 = sem("moved2")
        ones_set = sem("ones_set")
        ident_zero = sem("ident_zero")
        ident_set = sem("ident_set")
        ident16_set = sem("ident16_set")
        small_set = sem("small_set")
        spreader_set = sem("spreader_set")
        kmax2_set = sem("kmax2_set")
        kmax_set = sem("kmax_set")
        kmax_all_set = sem("kmax_all_set")
        kchain = sem("kchain")
        tanh_set = sem("tanh_set")
        gchain = sem("gchain")
        khl_high = sem("khl_high")
        khl_low = sem("khl_low")
        k_tr = sem("k_tr")
        k_high = sem("k_high")
        k_low = sem("k_low")
        w_tr = sem("w_tr")
        w_signed = sem("w_signed")
        abs_dve = sem("abs_dve")
        abs_act = sem("abs_act")
        alpha_in_set = sem("alpha_in_set")
        alpha_tr = sem("alpha_tr")
        alpha_set = sem("alpha_set")
        stats1 = sem("stats1")
        mv1_set = sem("mv1_set")
        ve1_set = sem("ve1_set")
        r1_set = sem("r1_set")
        mr1_set = sem("mr1_set")
        nm1_set = sem("nm1_set")
        factors_set = sem("factors_set")
        spread_full = sem("spread_full")
        spread_set = sem("spread_set")
        xs1_set = sem("xs1_set")
        turned1 = sem("turned1")
        q_high = sem("q_high")
        q_set = sem("q_set")
        scores_ready = sem("scores_ready")
        logits_set = sem("logits_set")
        max_set = sem("max_set")
        neg_max_set = sem("neg_max_set")
        ex_set = sem("ex_set")
        rec_set = sem("rec_set")
        coef_set = sem("coef_set")
        prob_high = sem("prob_high")
        prob_set = sem("prob_set")
        pt_full = sem("pt_full")
        pt_set = sem("pt_set")
        c_ready = sem("c_ready")
        x1_set = sem("x1_set")
        stats2 = sem("stats2")
        mv2_set = sem("mv2_set")
        ve2_set = sem("ve2_set")
        r2_set = sem("r2_set")
        mr2_set = sem("mr2_set")
        nm2_set = sem("nm2_set")
        xn2_set = sem("xn2_set")
        turned2 = sem("turned2")
        x1b_set = sem("x1b_set")
        x1_high = sem("x1_high")
        x1t_set = sem("x1t_set")
        y_ready = sem("y_ready")
        y_scaled = sem("y_scaled")
        y_added = sem("y_added")

        def chunk(n):
            return slice(n * BANK, (n + 1) * BANK)

        def columns(row, h):
            return row.rearrange("p (a h n) -> p h a n", a=4, h=2)[:, h]

        def laid_out(slot, h):
            return xr[:, slot, D // 2 * h:D // 2 * (h + 1)].rearrange("p (a n) -> p a n", a=4)

        def move_to_quadrants(queue, dst, src, moved):
            for a in range(4):
                queue.dma_start(dst[Q * a:Q * (a + 1), :], src[:, chunk(a)]).then_inc(moved, 16)

        def move_x1(queue, u):
            queue.wait_ge(xn2_set, u + 1)
            move_to_quadrants(queue, xs2, xn2, moved2)

        block = ctx.enter_context(nc.Block())

        @block.sync
        def _(sp):
            def load_quadrants(u):
                if not (isinstance(u, int) and u == 0):
                    sp.wait_ge(turned1, u)
                for a in range(4):
                    sp.dma_start(xs1[Q * a:Q * (a + 1), :].rearrange("p (c n) -> p c n", c=4),
                                 x_q[u, a]).then_inc(xs1_in, 16)

            sp.dma_start(xr[:, 0, :], x_t[0]).then_inc(x_in[0], 16)
            load_quadrants(0)
            for i in range(2):
                for h in range(2):
                    sp.dma_start(xr[:, 2 + i, D // 2 * h:D // 2 * (h + 1)].rearrange("p (a n) -> p a n", a=4),
                                 ctx_t[i, h]).then_inc(ctx_in[i], 16)
            sp.dma_start(gates[:, 0:1], g_xattn.partition_broadcast(P)).then_inc(consts_in, 16)
            sp.dma_start(gates[:, 1:2], g_ffn.partition_broadcast(P)).then_inc(consts_in, 16)

            def load_w(h):
                if h >= RW:
                    before = h - RW
                    sp.wait_ge(w_tr, 2 * before + 2)
                    if before % 2 == 0:
                        sp.wait_ge(abs_dve, before // 2 + 1)
                    else:
                        sp.wait_ge(abs_act, before // 2 + 1)
                sp.dma_start(wstage[:, h % RW, :].rearrange("p (a n) -> p a n", a=4),
                             w_t[h // 2, h % 2]).then_inc(w_in[h % RW], 16)

            def load_kt(batch):
                sp.dma_start(kt_cur[:, :, :].rearrange("p a b -> p (a b)"), kt_dram[batch]).then_inc(kt_in, 16)

            def load_kd(batch):
                sp.dma_start(kd_cur[:, :, :].rearrange("p a b -> p (a b)"), kd_dram[batch]).then_inc(kd_in, 16)

            for h in range(RW):
                load_w(h)
                if h == 1:
                    sp.dma_start(xr[:, 1, :], x_t[1]).then_inc(x_in[1], 16)
            sp.dma_start(bias_b[:, :], bias.partition_broadcast(P)).then_inc(bias_in, 16)
            sp.wait_ge(kts_stored[0], 16)
            load_kt(0)
            sp.wait_ge(khl_stored[0], 16 * 4)
            load_kd(0)
            load_quadrants(1)
            for i in range(2):
                load_w(RW + 2 * i)
                load_w(RW + 2 * i + 1)
                sp.wait_ge(k_tr, NG * (i + 1))
                sp.wait_ge(khl_low, i + 1)
                sp.dma_start(xr[:, 2 + i, :], x_t[2 + i]).then_inc(x_in[2 + i], 16)
            for h in range(RW + 4, 2 * NW):
                load_w(h)
                if h in (RW + 5, RW + 15):
                    load_quadrants(2 if h == RW + 5 else 3)
            load_quadrants(4)

            def store(u, r):
                sp.wait_ge(y_added, 7 if isinstance(u, int) and u == 0 else u * NC + NC)
                sp.dma_start(out_t[u], xr[:, r, :]).then_inc(out_done[r], 16)

            def reload(u, r, times):
                sp.wait_ge(out_done[r], times * 16)
                sp.dma_start(xr[:, r, :], x_t[u + RX]).then_inc(x_in[r], 16)

            store(0, 0)
            reload(0, 0, 1)
            move_x1(sp, 3)
            store(1, 1)
            load_quadrants(5)
            reload(1, 1, 1)
            move_x1(sp, 4)

            sp.wait_ge(kts_stored[1], 16)
            sp.wait_ge(khl_stored[1], 16 * 4)
            with sp.Fori(0, LOOPS) as i:
                for j in range(STEPS):
                    t, r = i * STEPS + (FIRST + j), (FIRST + j) % RX
                    store(t - 1, (r - 1) % RX)
                    reload(t - 1, (r - 1) % RX, i + (FIRST + j - 1) // RX + 1)
                    load_quadrants(t + 3)
                    if j == 2:
                        batch = (i + 2) // 2
                        sp.wait_ge(scores_ready, i * STEPS + 2 * STEPS)
                        load_kt(batch)
                        sp.wait_ge(c_ready, i * STEPS * NC + 2 * STEPS * NC)
                        load_kd(batch)
                    move_x1(sp, t + 2)
            for t in range(FIRST + STEPS * LOOPS, NT):
                store(t - 1, (t - 1) % RX)
                if t + 3 < NT:
                    reload(t - 1, (t - 1) % RX, (t - 1) // RX + 1)
                    load_quadrants(t + 3)
                if t + 2 < NT:
                    move_x1(sp, t + 2)
            store(NT - 1, (NT - 1) % RX)
            for r in range(RX):
                sp.wait_ge(out_done[r], 16 * (NT // RX))

        @block.gpsimd
        def _(pool):
            nc.gpsimd.memset(ident[:, :], 0.0).then_inc(ident_zero, 1)
            pool.wait_ge(ident_zero, 1)
            nc.gpsimd.affine_select(out=ident[:, :], in_=ident[:, :], compare_op=ALU.not_equal, fill=1.0, base=0,
                                    pattern=[[-1, P]], channel_multiplier=1).then_inc(ident_set, 1)
            nc.gpsimd.memset(neg_half[:, :], -0.5).then_inc(small_set, 1)
            nc.gpsimd.memset(eps[:, :], EPS).then_inc(small_set, 1)
            nc.gpsimd.memset(zero[:, :], 0.0).then_inc(small_set, 1)
            pool.wait_ge(small_set, 3)

            def rstd(u, mv, ve, r, mr, nm, mv_set, ve_set, r_set, mr_set, nm_set):
                pool.wait_ge(mv_set, u + 1)
                nc.gpsimd.tensor_tensor(ve[:, :], mv[:, 1:2], eps[:, :], ALU.add).then_inc(ve_set, 1)
                pool.wait_ge(ve_set, u + 1)
                nc.gpsimd.tensor_tensor(r[:, :], ve[:, :], neg_half[:, :], ALU.pow).then_inc(r_set, 1)
                pool.wait_ge(r_set, u + 1)
                nc.gpsimd.tensor_tensor(mr[:, :], mv[:, 0:1], r[:, :], ALU.mult).then_inc(mr_set, 1)
                pool.wait_ge(mr_set, u + 1)
                nc.gpsimd.tensor_tensor(nm[:, :], zero[:, :], mr[:, :], ALU.subtract).then_inc(nm_set, 1)

            def rstd1(u):
                rstd(u, mv1, ve1, r1, mr1, nm1, mv1_set, ve1_set, r1_set, mr1_set, nm1_set)

            def rstd2(u):
                rstd(u, mv2, ve2, r2, mr2, nm2, mv2_set, ve2_set, r2_set, mr2_set, nm2_set)

            def add_bias(u, r):
                pool.wait_ge(xn2_set, u + 1)
                nc.gpsimd.tensor_tensor(xr[:, r, :], xr[:, r, :], bias_b[:, :], ALU.add).then_inc(x1b_set, 1)

            rstd1(0)
            pool.wait_ge(kmax_set, 1)
            nc.gpsimd.partition_all_reduce(kmax_all[:, :], kmax[:, :], P, bass.bass_isa.ReduceOp.max).then_inc(kmax_all_set, 1)
            for i in range(2):
                pool.wait_ge(k_low, NG * (i + 1))
                pool.dma_start(kt_dram[2 * i:2 * i + 2].rearrange("b p n -> p b n"),
                               kts[i].rearrange("p b a k -> p b (a k)")).then_inc(kts_stored[i], 16)
                pool.wait_ge(khl_low, i + 1)
                for b in range(2):
                    for c in range(2):
                        pool.dma_start(kd_dram[2 * i + b, NKEY * c:NKEY * (c + 1), :],
                                       khl[NKEY * b:NKEY * (b + 1), i, :, :].rearrange("p a b -> p (a b)")).then_inc(khl_stored[i], 16)
            rstd1(1)
            pool.wait_ge(gchain, 3)
            for u in range(2):
                rstd2(u)
                add_bias(u, u)
            rstd1(2)
            rstd1(3)
            rstd2(2)
            add_bias(2, 2)
            rstd2(3)
            add_bias(3, 3)
            rstd1(4)
            rstd1(5)
            rstd2(4)
            add_bias(4, 0)

            def step(t, r, attention=True, ln1=True):
                if ln1:
                    rstd1(t + 3)
                if attention:
                    rstd2(t + 2)
                    add_bias(t + 2, (r + 2) % RX)

            with pool.Fori(0, LOOPS) as i:
                for j in range(STEPS):
                    step(i * STEPS + (FIRST + j), (FIRST + j) % RX)
            for t in range(FIRST + STEPS * LOOPS, NT):
                step(t, t % RX, attention=t + 2 < NT, ln1=t + 3 < NT)

        @block.scalar
        def _(act):
            def normalise1(u):
                act.wait_ge(spread_full, u + 1)
                nc.scalar.copy(spread[:, :, :].rearrange("p a b -> p (a b)"), s_ps[:, 0:8]).then_inc(spread_set, 1)
                act.wait_ge(spread_set, u + 1)
                act.wait_ge(xs1_in, u * 64 + 64)
                for c in range(4):
                    last = nc.scalar.activation(xs1[:, chunk(c)], xs1[:, chunk(c)], ACT.Identity,
                                                bias=spread[:, 1, c:c + 1], scale=spread[:, 0, c:c + 1])
                last.then_inc(xs1_set, 1)

            def normalise2(u, r):
                act.wait_ge(nm2_set, u + 1)
                if not (isinstance(u, int) and u == 0):
                    act.wait_ge(x1t_set, u)
                nc.scalar.activation(xn2[:, :], xr[:, r, :], ACT.Identity, bias=nm2[:, :],
                                     scale=r2[:, :]).then_inc(xn2_set, 1)

            def high_q(u):
                act.wait_ge(turned1, u + 1)
                if not (isinstance(u, int) and u == 0):
                    act.wait_ge(scores_ready, u)
                nc.scalar.activation(qt[:, 0, :], xn1[:, :], ACT.Copy, scale=LN_SCALE).then_inc(q_high, 1)

            def high_x1(u, slot):
                act.wait_ge(turned2, u + 1)
                if not isinstance(u, int) or u >= 3:
                    act.wait_ge(y_ready, u * NC - NC)
                elif u == 2:
                    act.wait_ge(y_ready, 7)
                nc.scalar.activation(x1t[:, slot, 0, :], xn2[:, :], ACT.Copy, scale=LN_SCALE).then_inc(x1_high, 1)

            def exp(u):
                act.wait_ge(neg_max_set, u + 1)
                nc.scalar.activation(ex[:, :], logits[:, :], ACT.Exp, bias=neg_max[:, :], scale=lscale[:, :],
                                     accum_out=sum_ex[:, :]).then_inc(ex_set, 1)

            def copy_pt(u):
                if not (isinstance(u, int) and u == 0):
                    act.wait_ge(c_ready, u * NC)
                act.wait_ge(pt_full, u + 1)
                nc.scalar.copy(pt[:, :], pt_ps).then_inc(pt_set, 1)

            def sign_group(m):
                w, g = m // NG, m % NG
                act.wait_ge(w_tr, m + 1)
                nc.scalar.activation(wsign[:, GROUP * g:GROUP * (g + 1), P * w:P * (w + 1)],
                                     setup_ps[:, setup_order.index(("w", m)) % RB, :].rearrange("p (a b) -> p a b", a=GROUP),
                                     ACT.Sign).then_inc(w_signed, 1)

            def abs_half(h):
                act.wait_ge(w_in[h % RW], 16 * (h // RW + 1))
                act.wait_ge(w_tr, 2 * h + 2)
                nc.scalar.activation(wstage[:, h % RW, :], wstage[:, h % RW, :], ACT.Abs,
                                     accum_out=abs_sum[:, h:h + 1]).then_inc(abs_act, 1)

            def sign_tile(w):
                for m in range(NG * w, NG * (w + 1)):
                    sign_group(m)
                abs_half(2 * w + 1)

            def key_high(i, g):
                act.wait_ge(k_tr, NG * i + g + 1)
                src = setup_ps[:, setup_order.index(("keys", NG * i + g)) % RB, :].rearrange(
                    "p (a b k) -> p b a k", a=GROUP, b=2)
                for b in range(2):
                    last = nc.scalar.activation(kts[i][:, b, GROUP * g:GROUP * (g + 1), 0:NKEY], src[:, b], ACT.Copy,
                                                scale=kscale[:, :])
                last.then_inc(k_high, 1)

            act.wait_ge(consts_in, 32)
            nc.scalar.activation(tanh_g[:, :], gates[:, :], ACT.Tanh).then_inc(tanh_set, 1)
            normalise1(0)
            act.wait_ge(kchain, 4)
            for i in range(2):
                for g in range(NG):
                    key_high(i, g)
                act.wait_ge(ctx_in[i], 32)
                for h in range(2):
                    last = nc.scalar.activation(columns(khl[:, i, 0, :], h), laid_out(2 + i, h), ACT.Copy,
                                                scale=kscale[:, :])
                last.then_inc(khl_high, 1)
                if i == 0:
                    high_q(0)
            sign_tile(0)
            sign_tile(1)
            normalise1(1)
            exp(0)
            sign_tile(2)
            high_q(1)
            copy_pt(0)
            sign_tile(3)
            act.wait_ge(kts_stored[1], 16)
            normalise2(0, 0)
            move_x1(act, 0)
            exp(1)
            copy_pt(1)
            act.wait_ge(khl_stored[0], 16 * 4)
            high_x1(0, 0)
            normalise2(1, 1)
            move_x1(act, 1)
            act.wait_ge(khl_stored[1], 16 * 4)
            high_x1(1, 1)

            for k in range(PAIR_BLOCKS):
                if k < 24:
                    sign_group(CHUNK_GROUPS + 2 * k)
                    sign_group(CHUNK_GROUPS + 1 + 2 * k)
                    if k % 2 == 1:
                        abs_half(2 * (GROUP + k // 2) + 1)
                if k in PAIR_SPREAD:
                    normalise1(PAIR_SPREAD[k])
                if k in (6, 18):
                    high_q(2 if k == 6 else 3)
                if k in PAIR_SCORES:
                    exp(PAIR_SCORES[k])
                if k in PAIR_PT:
                    copy_pt(PAIR_PT[k])
                if k == 16:
                    normalise2(2, 2)
                    move_x1(act, 2)
                if k == 28:
                    high_x1(2, 0)
            normalise2(3, 3)

            normalise1(4)
            high_x1(3, 1)
            high_q(4)
            exp(4)
            copy_pt(4)
            normalise1(5)
            normalise2(4, 0)
            high_q(5)

            def step(t, r, x1=True, attention=True, ln1=True):
                if x1:
                    high_x1(t + 1, (r + 1) % 2)
                if attention:
                    exp(t + 2)
                    copy_pt(t + 2)
                if ln1:
                    normalise1(t + 3)
                if attention:
                    normalise2(t + 2, (r + 2) % RX)
                if ln1:
                    high_q(t + 3)

            with act.Fori(0, LOOPS) as i:
                for j in range(STEPS):
                    step(i * STEPS + (FIRST + j), (FIRST + j) % RX)
            for t in range(FIRST + STEPS * LOOPS, NT):
                step(t, t % RX, x1=t + 1 < NT, attention=t + 2 < NT, ln1=t + 3 < NT)

        @block.vector
        def _(dve):
            def norm_stats1(u, r, n):
                if n == 0:
                    dve.wait_ge(x_in[r], (u - r) * (16 // RX) + 16)
                nc.vector.bn_stats(st1[:, n, :], xr[:, r, chunk(n)]).then_inc(stats1, 1)

            def stats1_done(u):
                dve.wait_ge(stats1, u * NC + NC)

            def norm_mean1(u):
                nc.vector.bn_aggr(mv1[:, :], st1[:, :, :].rearrange("p a b -> p (a b)")).then_inc(mv1_set, 1)

            def stats2_done(u):
                dve.wait_ge(stats2, u * NC + NC)

            def norm_mean2(u):
                nc.vector.bn_aggr(mv2[:, :], st2[:, :, :].rearrange("p a b -> p (a b)")).then_inc(mv2_set, 1)

            def ln1_mean(u, r):
                for n in range(NC):
                    norm_stats1(u, r, n)
                stats1_done(u)
                norm_mean1(u)

            def turn(dst, src):
                for h in range(2):
                    last = nc.vector.transpose(
                        dst[:, D // 2 * h:D // 2 * (h + 1)].rearrange("p (k i c) -> p k c i", k=8, c=4),
                        src[:, :].rearrange("p (c h j k) -> p h k c j", c=4, h=2, j=Q)[:, h])
                return last

            def place_factors(u):
                dve.wait_ge(nm1_set, u + 1)
                nc.vector.tensor_scalar(factors[:, 0, :], own_c[:, :], r1[:, 0:1], None, ALU.mult)
                nc.vector.tensor_scalar(factors[:, 1, :], own_c[:, :], nm1[:, 0:1], None, ALU.mult).then_inc(factors_set, 1)

            def turn_q(u):
                dve.wait_ge(xs1_set, u + 1)
                turn(xn1, xs1).then_inc(turned1, 1)

            def turn_x1(u):
                dve.wait_ge(moved2, u * 64 + 64)
                turn(xn2, xs2).then_inc(turned2, 1)

            def low_q(u):
                dve.wait_ge(q_high, u + 1)
                nc.vector.scalar_tensor_tensor(out=qt[:, 1, :], in0=xn1[:, :], scalar=LN_SCALE, in1=qt[:, 0, :],
                                               op0=ALU.mult, op1=ALU.subtract).then_inc(q_set, 1)

            def low_x1(u, slot):
                dve.wait_ge(x1_high, u + 1)
                nc.vector.scalar_tensor_tensor(out=x1t[:, slot, 1, :], in0=xn2[:, :], scalar=LN_SCALE,
                                               in1=x1t[:, slot, 0, :], op0=ALU.mult, op1=ALU.subtract).then_inc(x1t_set, 1)

            def max_logits(u):
                dve.wait_ge(scores_ready, u + 1)
                nc.vector.tensor_reduce(logits[:, :], s_ps[:, 0:P].rearrange("p (h k) -> p k h", h=2), X,
                                        ALU.add).then_inc(logits_set, 1)
                dve.wait_ge(logits_set, u + 1)
                nc.vector.tensor_reduce(row_max[:, :], logits[:, :], X, ALU.max).then_inc(max_set, 1)
                dve.wait_ge(max_set, u + 1)
                nc.vector.tensor_scalar(neg_max[:, :], row_max[:, :], neg_lscale[:, 0:1], None,
                                        ALU.mult).then_inc(neg_max_set, 1)

            def split_probs(u):
                dve.wait_ge(ex_set, u + 1)
                nc.vector.tensor_scalar(prob[:, 0, :], ex[:, :], PROB_SCALE, None, ALU.mult).then_inc(prob_high, 1)
                nc.vector.reciprocal(rec_ex[:, :], sum_ex[:, :]).then_inc(rec_set, 1)
                dve.wait_ge(prob_high, u + 1)
                nc.vector.scalar_tensor_tensor(out=prob[:, 1, :], in0=ex[:, :], scalar=PROB_SCALE, in1=prob[:, 0, :],
                                               op0=ALU.mult, op1=ALU.subtract).then_inc(prob_set, 1)
                dve.wait_ge(rec_set, u + 1)
                nc.vector.tensor_scalar(coef[:, :], rec_ex[:, :], gx[:, 0:1], None, ALU.mult).then_inc(coef_set, 1)

            def add_attention(u, r, n):
                dve.wait_ge(c_ready, u * NC + (n + 1))
                if n == 0:
                    dve.wait_ge(coef_set, u + 1)
                nc.vector.scalar_tensor_tensor(out=xr[:, r, chunk(n)], in0=c_ps[:, n % 2, :], scalar=coef[:, 0:1],
                                               in1=xr[:, r, chunk(n)], op0=ALU.mult, op1=ALU.add).then_inc(x1_set, 1)

            def norm_stats2(u, r, n):
                dve.wait_ge(x1_set, u * NC + (n + 1))
                nc.vector.bn_stats(st2[:, n, :], xr[:, r, chunk(n)]).then_inc(stats2, 1)

            def scale_y(t, n, r):
                k = seq_y(t, n)
                bank = (t if isinstance(t, int) and t < 2 else n) % 2
                dve.wait_ge(y_ready, k + 1)
                nc.vector.tensor_tensor(ytmp[:, bank, :], y_ps[:, bank, :], alpha_b[:, chunk(n)],
                                        ALU.mult).then_inc(y_scaled, 1)

            def add_y(t, n, r):
                k = seq_y(t, n)
                bank = (t if isinstance(t, int) and t < 2 else n) % 2
                dve.wait_ge(y_scaled, k + 1)
                dve.wait_ge(x1b_set, t + 1)
                nc.vector.tensor_tensor(xr[:, r, chunk(n)], ytmp[:, bank, :], xr[:, r, chunk(n)],
                                        ALU.add).then_inc(y_added, 1)

            def finish_y(t, n, r):
                scale_y(t, n, r)
                add_y(t, n, r)

            def sum_abs(w):
                h = 2 * w
                dve.wait_ge(w_in[h % RW], 16 * (h // RW + 1))
                nc.vector.tensor_reduce(abs_sum[:, h:h + 1], wstage[:, h % RW, :], X, ALU.add,
                                        apply_absolute_value=True).then_inc(abs_dve, 1)

            def spread_alpha(w):
                dve.wait_ge(abs_dve, w + 1)
                dve.wait_ge(abs_act, w + 1)
                if w >= GROUP:
                    dve.wait_ge(alpha_tr, w // GROUP)
                nc.vector.tensor_scalar(alpha_in[:, w % GROUP, :], ones[:, :], abs_sum[:, 2 * w:2 * w + 1],
                                        abs_sum[:, 2 * w + 1:2 * w + 2], ALU.mult, ALU.add).then_inc(alpha_in_set, 1)

            def take_alpha(n):
                dve.wait_ge(alpha_tr, n + 1)
                nc.vector.tensor_scalar(alpha_b[:, chunk(n)], setup_ps[:, setup_order.index(("alpha", n)) % RB, :],
                                        gy[:, 0:1], None, ALU.mult).then_inc(alpha_set, 1)

            def key_low(i, g):
                dve.wait_ge(k_high, NG * i + g + 1)
                src = setup_ps[:, setup_order.index(("keys", NG * i + g)) % RB, :].rearrange(
                    "p (a b k) -> p b a k", a=GROUP, b=2)
                for b in range(2):
                    dst = kts[i][:, b, GROUP * g:GROUP * (g + 1), :]
                    last = nc.vector.scalar_tensor_tensor(out=dst[:, :, NKEY:], in0=src[:, b], scalar=kscale[:, 0:1],
                                                          in1=dst[:, :, 0:NKEY], op0=ALU.mult, op1=ALU.subtract)
                last.then_inc(k_low, 1)

            nc.vector.memset(ones[:, :], 1.0).then_inc(ones_set, 1)
            ln1_mean(0, 0)
            dve.wait_ge(ident_set, 1)
            nc.vector.tensor_reduce(own_c[:, :], ident[:, :].rearrange("p (i c) -> p c i", c=4), X,
                                    ALU.add).then_inc(spreader_set, 1)
            for a in range(4):
                nc.vector.tensor_reduce(same_i[:, Q * a:Q * (a + 1)], ident[:, :].rearrange("p (i c) -> p i c", c=4), X,
                                        ALU.add).then_inc(spreader_set, 1)
            dve.wait_ge(spreader_set, 5)
            place_factors(0)
            for i in range(2):
                dve.wait_ge(ctx_in[i], 32)
                nc.vector.tensor_reduce(kmax2[:, i:i + 1], xr[:, 2 + i, :], X, ALU.max,
                                        apply_absolute_value=True).then_inc(kmax2_set, 1)
            dve.wait_ge(kmax2_set, 2)
            nc.vector.tensor_reduce(kmax[:, :], kmax2[:, :], X, ALU.max).then_inc(kmax_set, 1)
            dve.wait_ge(kmax_all_set, 1)
            nc.vector.tensor_scalar(kpow[:, :].bitcast(I32), kmax_all[:, :].bitcast(I32), 0x7F800000, None,
                                    ALU.bitwise_and).then_inc(kchain, 1)
            dve.wait_ge(kchain, 1)
            nc.vector.tensor_scalar(kinv[:, :], kpow[:, :], 2.0 ** -90, 1.0 / KEY_TOP, ALU.max, ALU.mult).then_inc(kchain, 1)
            dve.wait_ge(kchain, 2)
            nc.vector.reciprocal(kscale[:, :], kinv[:, :]).then_inc(kchain, 1)
            dve.wait_ge(kchain, 3)
            nc.vector.tensor_scalar(lscale[:, :], kinv[:, :], 1.0 / LN_SCALE, None, ALU.mult).then_inc(kchain, 1)
            nc.vector.tensor_scalar(neg_lscale[:, :], kinv[:, :], -1.0 / LN_SCALE, None, ALU.mult).then_inc(kchain, 1)
            dve.wait_ge(tanh_set, 1)
            nc.vector.tensor_scalar(gx[:, :], tanh_g[:, 0:1], kinv[:, 0:1], 1.0 / PROB_SCALE, ALU.mult,
                                    ALU.mult).then_inc(gchain, 1)
            nc.vector.tensor_scalar(gy[:, :], tanh_g[:, 1:2], 1.0 / (D * LN_SCALE), None, ALU.mult).then_inc(gchain, 1)
            dve.wait_ge(kchain, 5)
            dve.wait_ge(gchain, 2)
            for i in range(2):
                for g in range(NG):
                    key_low(i, g)
                if i == 0:
                    turn_q(0)
                dve.wait_ge(khl_high, i + 1)
                for h in range(2):
                    last = nc.vector.scalar_tensor_tensor(
                        out=columns(khl[:, i, 1, :], h), in0=laid_out(2 + i, h), scalar=kscale[:, 0:1],
                        in1=columns(khl[:, i, 0, :], h), op0=ALU.mult, op1=ALU.subtract)
                last.then_inc(khl_low, 1)
                if i == 0:
                    low_q(0)
            nc.vector.tensor_copy(ident16[:, :], ident[:, :]).then_inc(ident16_set, 1)
            ln1_mean(1, 1)
            sum_abs(0)
            place_factors(1)
            sum_abs(1)
            dve.wait_ge(bias_in, 16)
            nc.vector.tensor_scalar(bias_b[:, :], bias_b[:, :], tanh_g[:, 1:2], None, ALU.mult).then_inc(gchain, 1)
            max_logits(0)
            split_probs(0)
            sum_abs(2)
            turn_q(1)
            low_q(1)
            dve.wait_ge(ones_set, 1)
            spread_alpha(0)
            spread_alpha(1)
            for n in range(NC):
                add_attention(0, 0, n)
                norm_stats2(0, 0, n)
            stats2_done(0)
            norm_mean2(0)
            max_logits(1)
            sum_abs(3)
            split_probs(1)
            spread_alpha(2)
            spread_alpha(3)
            for n in range(NC):
                add_attention(1, 1, n)
                norm_stats2(1, 1, n)
            stats2_done(1)
            norm_mean2(1)
            turn_x1(0)
            low_x1(0, 0)
            take_alpha(0)
            turn_x1(1)
            low_x1(1, 1)

            for k in range(PAIR_BLOCKS):
                if k < 24 and k % 2 == 0:
                    sum_abs(GROUP + k // 2)
                if k < 24 and k % 2 == 1:
                    spread_alpha(GROUP + k // 2)
                if k in (1, 13):
                    u = 2 if k == 1 else 3
                    ln1_mean(u, u)
                if k in (2, 14):
                    place_factors(2 if k == 2 else 3)
                if k in (5, 17):
                    turn_q(2 if k == 5 else 3)
                if k in (6, 18):
                    low_q(2 if k == 6 else 3)
                if k in PAIR_SCORES:
                    max_logits(PAIR_SCORES[k])
                    split_probs(PAIR_SCORES[k])
                if k in PAIR_C:
                    u, n = PAIR_C[k]
                    add_attention(u, u, n)
                    norm_stats2(u, u, n)
                    if n == NC - 1:
                        stats2_done(u)
                        norm_mean2(u)
                if k in PAIR_ALPHA:
                    take_alpha(PAIR_ALPHA[k])
                if k % 4 == 3 and k < 31:
                    if k % 8 == 3:
                        dve.wait_ge(alpha_set, k // 8 + 1)
                    finish_y(k // 4 % 2, k // 8, k // 4 % 2)
                if k == 26:
                    turn_x1(2)
                if k == 28:
                    low_x1(2, 0)

            finish_y(1, 3, 1)
            ln1_mean(4, 0)
            finish_y(2, 0, 2)
            place_factors(4)
            turn_x1(3)
            turn_q(4)
            low_x1(3, 1)
            low_q(4)
            finish_y(2, 1, 2)
            ln1_mean(5, 1)
            place_factors(5)
            max_logits(4)
            split_probs(4)
            finish_y(2, 2, 2)
            for n in range(NC):
                add_attention(4, 0, n)
                norm_stats2(4, 0, n)
            stats2_done(4)
            norm_mean2(4)
            turn_q(5)
            low_q(5)

            def step(t, r, x1=True, attention=True, ln1=True):
                a, ra = t + 2, (r + 2) % RX
                a1, ra1 = t + 3, (r + 3) % RX
                finish_y(t - 1, 3, (r - 1) % RX)
                if x1:
                    turn_x1(t + 1)
                if attention:
                    max_logits(a)
                    split_probs(a)
                if x1:
                    low_x1(t + 1, (r + 1) % 2)
                if ln1:
                    for n in range(NC):
                        norm_stats1(a1, ra1, n)
                    stats1_done(a1)
                scale_y(t, 0, r)
                if ln1:
                    norm_mean1(a1)
                add_y(t, 0, r)
                for n in range(NC):
                    if attention:
                        add_attention(a, ra, n)
                        norm_stats2(a, ra, n)
                    if ln1 and n == 0:
                        place_factors(a1)
                if attention:
                    stats2_done(a)
                scale_y(t, 1, r)
                if attention:
                    norm_mean2(a)
                add_y(t, 1, r)
                if ln1:
                    turn_q(a1)
                finish_y(t, 2, r)
                if ln1:
                    low_q(a1)

            with dve.Fori(0, LOOPS) as i:
                for j in range(STEPS):
                    step(i * STEPS + (FIRST + j), (FIRST + j) % RX)
            for t in range(FIRST + STEPS * LOOPS, NT):
                step(t, t % RX, x1=t + 1 < NT, attention=t + 2 < NT, ln1=t + 3 < NT)
            finish_y(NT - 1, 3, (NT - 1) % RX)

        @block.tensor
        def _(pe):
            def through_bank(kind, src, done):
                n = setup_order.index(kind)
                if n >= RB:
                    what, m = setup_order[n - RB]
                    pe.wait_ge({"keys": k_low, "w": w_signed, "alpha": alpha_set}[what], m + 1)
                for b in range(GROUP):
                    last = nc.tensor.transpose(setup_ps[:, n % RB, P * b:P * (b + 1)], src(b), ident[:, :])
                last.then_inc(done, 1)

            def transpose_keys(i, g):
                if g == 0:
                    pe.wait_ge(ctx_in[i], 32)
                rows = xr[:, 2 + i, D // 2 * (g // 2):D // 2 * (g // 2 + 1)].rearrange("p (m k) -> p k m", k=8)
                through_bank(("keys", NG * i + g), lambda b: rows[:, GROUP * (g % 2) + b], k_tr)

            def transpose_w(m):
                h = m // 2
                if m % 2 == 0:
                    pe.wait_ge(w_in[h % RW], 16 * (h // RW + 1))
                rows = wstage[:, h % RW, :].rearrange("p (m k) -> p k m", k=8)
                through_bank(("w", m), lambda b: rows[:, GROUP * (m % 2) + b], w_tr)

            def transpose_alpha(n):
                pe.wait_ge(alpha_in_set, GROUP * (n + 1))
                through_bank(("alpha", n), lambda b: alpha_in[:, b, :], alpha_tr)

            def spread_factors(u):
                if isinstance(u, int) and u == 0:
                    pe.wait_ge(spreader_set, 5)
                pe.wait_ge(factors_set, u + 1)
                nc.tensor.matmul(s_ps[:, 0:8], same_i[:, :], factors[:, :, :].rearrange("p a b -> p (a b)"), start=True,
                                 stop=True).then_inc(spread_full, 1)

            def scores(u):
                pe.wait_ge(q_set, u + 1)
                for k in range(ND):
                    for part in range(2):
                        last = nc.tensor.matmul(s_ps[:, 0:P], qt[:, part, P * k:P * (k + 1)], kt_cur[:, k, :],
                                                start=(k == 0 and part == 0), stop=(k == ND - 1 and part == 1))
                last.then_inc(scores_ready, 1)

            def transpose_probs(u):
                pe.wait_ge(prob_set, u + 1)
                nc.tensor.transpose(pt_ps, prob[:, :, :].rearrange("p a b -> p (a b)"), ident16[:, :]).then_inc(pt_full, 1)

            def attend(u, n):
                if n == 0:
                    pe.wait_ge(pt_set, u + 1)
                if not (isinstance(u, int) and u == 0 and n < 2):
                    pe.wait_ge(x1_set, u * NC + (n - 1))
                for part in range(2):
                    last = nc.tensor.matmul(c_ps[:, n % 2, :], pt[:, :], kd_cur[:, part, chunk(n)],
                                            start=(part == 0), stop=(part == 1))
                last.then_inc(c_ready, 1)

            def ffn_block(bank, slot, n, q):
                for k in range(4 * q, 4 * q + 4):
                    for part in range(2):
                        last = nc.tensor.matmul(y_ps[:, bank, :], x1t[:, slot, part, P * k:P * (k + 1)],
                                                wsign[:, k, chunk(n)], start=(k == 0 and part == 0),
                                                stop=(k == ND - 1 and part == 1))
                if q == 3:
                    last.then_inc(y_ready, 1)

            spread_factors(0)
            pe.wait_ge(ident_set, 1)
            for i in range(2):
                for g in range(NG):
                    transpose_keys(i, g)
            for m in range(8):
                transpose_w(m)
            pe.wait_ge(spread_set, 1)
            spread_factors(1)
            pe.wait_ge(kt_in, 16)
            pe.wait_ge(spread_set, 2)
            scores(0)
            for m in range(8, 12):
                transpose_w(m)
            pe.wait_ge(ident16_set, 1)
            transpose_probs(0)
            pe.wait_ge(kd_in, 16)
            for n in range(NC):
                attend(0, n)
                transpose_w(12 + n)
            scores(1)
            transpose_probs(1)
            for n in range(NC):
                attend(1, n)
            transpose_alpha(0)

            for k in range(PAIR_BLOCKS):
                n, tile, q = k // 8, k // 4 % 2, k % 4
                if q == 0:
                    if tile == 0:
                        pe.wait_ge(w_signed, CHUNK_GROUPS * (n + 1))
                    if n == 0:
                        pe.wait_ge(x1t_set, tile + 1)
                    if n > 0:
                        pe.wait_ge(y_scaled, 2 * n + tile - 1)
                ffn_block(tile, tile, n, q)
                if k < 24:
                    transpose_w(CHUNK_GROUPS + 2 * k)
                    transpose_w(CHUNK_GROUPS + 1 + 2 * k)
                if k in PAIR_ALPHA:
                    transpose_alpha(PAIR_ALPHA[k])
                if k in PAIR_SPREAD:
                    spread_factors(PAIR_SPREAD[k])
                if k in PAIR_SCORES:
                    scores(PAIR_SCORES[k])
                if k in PAIR_PT:
                    transpose_probs(PAIR_PT[k])
                if k in PAIR_C:
                    attend(*PAIR_C[k])

            def step(t, r, attention=True, ln1=True, keys=None, late=False):
                scores_at, pt_at, c_at, spread_at = (
                    (LATE_SCORES_AT, LATE_PT_AT, LATE_C_AT, LATE_SPREAD_AT) if late else (SCORES_AT, PT_AT, C_AT, SPREAD_AT))
                pe.wait_ge(x1t_set, t + 1)
                for k in range(BLOCKS):
                    n, q = k // 4, k % 4
                    if q == 0:
                        pe.wait_ge(y_scaled, t * NC + (n - 1))
                    ffn_block(n % 2, r % 2, n, q)
                    if late and k == LATE_FIRST_SPREAD_AT:
                        spread_factors(t + 2)
                    if ln1 and k == spread_at:
                        spread_factors(t + 3)
                    if attention:
                        if k == scores_at:
                            if keys is not None:
                                pe.wait_ge(kt_in, keys)
                            scores(t + 2)
                        if k == pt_at:
                            transpose_probs(t + 2)
                        if k in c_at:
                            if c_at[k] == 0 and keys is not None:
                                pe.wait_ge(kd_in, keys)
                            attend(t + 2, c_at[k])

            step(2, 2, late=True)
            with pe.Fori(0, LOOPS) as i:
                for j in range(STEPS):
                    step(i * STEPS + (FIRST + j), (FIRST + j) % RX, keys=i * 16 + 32 if j == 3 else None)
            for t in range(FIRST + STEPS * LOOPS, NT):
                step(t, t % RX, attention=t + 2 < NT, ln1=t + 3 < NT)


_INS = ['x', 'ctx_4096', 'g_xattn', 'g_ffn', 'L0_ffn_weight_real', 'L0_ffn_bias']
_OUTS = [((4, 1024, 2048), 'float32')]


def kernel(**inputs):
    import numpy as _np
    import concourse.bacc as _bacc
    from concourse import mybir as _mybir
    from concourse.bass_utils import run_bass_kernel_spmd as _run

    nc = _bacc.Bacc("TRN2", target_bir_lowering=False, num_devices=1)
    arrays, args = {}, []
    for name in _INS:
        a = _np.ascontiguousarray(inputs[name])
        arrays[f"in_{name}_dram"] = a
        args.append(nc.dram_tensor(f"in_{name}_dram", a.shape, _mybir.dt.from_np(a.dtype), kind="ExternalInput").ap())
    for i, (shape, dtype) in enumerate(_OUTS):
        dt = _mybir.dt.from_np(_np.dtype(dtype))
        args.append(nc.dram_tensor(f"out_{i}_dram", shape, dt, kind="ExternalOutput").ap())
    flamingo_gated_kernel(nc, *args)
    r = _run(nc, [arrays], core_ids=[0])
    got = tuple(r.results[0][f"out_{i}_dram"] for i in range(len(_OUTS)))
    return got[0]
```

```python
import concourse.bass as bass
from concourse import mybir
from contextlib import ExitStack

P = 128
BANK = 512
GROUP = BANK // P
LN_SCALE = 2.0 ** 10
PROB_SCALE = 2.0 ** 14
KEY_TOP = 2.0 ** 14
EPS = 1e-5


def flamingo_gated_kernel(
    nc: bass.Bass,
    x: bass.AP,
    ctx_keys: bass.AP,
    g_xattn: bass.AP,
    g_ffn: bass.AP,
    weight: bass.AP,
    bias: bass.AP,
    out: bass.AP,
):
    F32, F16, I32 = mybir.dt.float32, mybir.dt.float16, mybir.dt.int32
    ALU = mybir.AluOpType
    ACT = mybir.ActivationFunctionType
    X = mybir.AxisListType.X

    NB, S, D = x.shape
    NKEY = ctx_keys.shape[1]
    DO = weight.shape[0]
    NT = NB * S // P
    ND = D // P
    NC = D // BANK
    NG = ND // GROUP
    Q = P // 4
    NW = DO // P
    TILES_PER_BATCH = S // P
    RX, RW, RB = 4, 4, 3
    STEPS = 4
    FIRST = 4
    LOOPS = (NT - 4 - FIRST) // STEPS
    BLOCKS = 16
    assert NKEY * 2 == P and D == DO and NC == 4 and NG == 4 and NB == 4
    assert TILES_PER_BATCH == 2 * STEPS and NT == FIRST + STEPS * LOOPS + 4

    x_t = x.rearrange("b (t p) d -> (b t) p d", p=P)
    x_q = x.rearrange("b (t i c) (a n) -> (b t) a i c n", c=4, i=Q, a=4)
    out_t = out.rearrange("b (t p) d -> (b t) p d", p=P)
    ctx_t = ctx_keys.rearrange("(i b) k (a h n) -> i h (b k) a n", b=2, a=4, h=2)
    w_t = weight.rearrange("(t p) (a h n) -> t h p a n", p=P, a=4, h=2)

    SCORES_AT, PT_AT, C_AT, SPREAD_AT = 2, 4, {6: 0, 7: 1, 8: 2, 9: 3}, 8
    LATE_SCORES_AT, LATE_PT_AT, LATE_C_AT, LATE_SPREAD_AT = 10, 11, {12: 0, 13: 1, 14: 2, 15: 3}, 13
    LATE_FIRST_SPREAD_AT = 4
    STEP3_SPREAD_AT = 9
    PAIR_BLOCKS = 32
    PAIR_ORDER = [(0, 0), (0, 1), (1, 0), (1, 1), (0, 2), (1, 2), (0, 3), (1, 3)]
    FINISHED_0 = PAIR_ORDER.index((0, NC - 1)) + 1
    PAIR_STATS = {9: 2, 15: 3}
    PAIR_PLACE = {10: 2, 16: 3}
    PAIR_SPREAD = {11: 2, 19: 3}
    PAIR_TURN = {13: 2, 22: 3}
    PAIR_SPLIT = {13: 2, 23: 3}
    PAIR_SCORES = {16: 2, 25: 3}
    PAIR_PT = {18: 2, 27: 3}
    PAIR_C = {19: (2, 0), 20: (2, 1), 21: (2, 2), 22: (2, 3), 28: (3, 0), 29: (3, 1), 30: (3, 2), 31: (3, 3)}
    PAIR_ALPHA = {1: 0, 6: 1, 18: 2, 24: 3}
    BEFORE_W = 20
    PAIR_W_COUNT = [3, 3, 3, 3, 3, 0, 1, 1, 3, 1, 2, 1, 2, 1, 1, 1, 2, 2, 1, 2, 2, 2, 2, 2] + [0] * 8
    PAIR_KEYS = {2: (0, 1, 2), 3: (3,)}
    PAIR_KEY_ROWS = 4
    NORM2_1, TURN_X1_1, LOW_X1_1 = 1, 3, 4
    NORM2_2, TURN_X1_2, LOW_X1_2 = 23, 27, 29
    BIAS_H, MOVE0_H, QUADRANTS2_H, MOVE1_H, X2_H, X3_H, QUADRANTS3_H = 5, 7, 10, 15, 20, 21, 27
    CHUNK_GROUPS = NG * GROUP

    setup_order = [("keys", n) for n in range(NG)] + [("w", m) for m in range(BEFORE_W)]
    pair_w = [range(BEFORE_W + sum(PAIR_W_COUNT[:k]), BEFORE_W + sum(PAIR_W_COUNT[:k + 1])) for k in range(PAIR_BLOCKS)]
    for k in range(PAIR_BLOCKS):
        setup_order += [("w", m) for m in pair_w[k]] + [("keys", NG + g) for g in PAIR_KEYS.get(k, ())]
        if k in PAIR_ALPHA:
            setup_order += [("alpha", PAIR_ALPHA[k])]

    def seq_y(t, n):
        return PAIR_ORDER.index((t, n)) if isinstance(t, int) and t < 2 else t * 4 + n

    with ExitStack() as ctx:
        def sb(name, shape, dt=F32):
            return ctx.enter_context(nc.sbuf_tensor(name, shape, dt))

        def psum(name, shape):
            return ctx.enter_context(nc.psum_tensor(name, shape, F32))

        def sem(name):
            return ctx.enter_context(nc.semaphore(name))

        kt_dram = nc.dram_tensor("kt_dram", [NB - 1, P, ND * P], F16, kind="Internal").ap()
        kd_dram = nc.dram_tensor("kd_dram", [NB - 1, NKEY, 2 * D], F16, kind="Internal").ap()

        wsign = sb("wsign", [P, ND, DO], F16)
        alpha_b = sb("alpha_b", [P, DO])
        bias_b = sb("bias_b", [P, DO])
        kt_cur = sb("kt_cur", [P, ND, P], F16)
        kd_cur = sb("kd_cur", [P, 2, D], F16)
        xr = sb("xr", [P, RX, D])
        x1t = sb("x1t", [P, 2, 2, D], F16)
        qt = sb("qt", [P, 2, D], F16)
        xs1 = sb("xs1", [P, D])
        xn1 = sb("xn1", [P, D])
        xn2 = sb("xn2", [P, D])
        xs2 = sb("xs2", [P, D])
        factors = sb("factors", [P, 2, 4])
        spread = sb("spread", [P, 2, 4])
        same_i = sb("same_i", [P, P])
        own_c = sb("own_c", [P, 4])
        ytmp = sb("ytmp", [P, 2, BANK])
        wstage = sb("wstage", [P, RW, D // 2])
        kts = [b.bitcast(F16).rearrange("p (b a k) -> p b a k", b=2, a=ND) for b in (xn2[:, :], xr[:, 2, :])]
        khl = [x1t[:, 0], xn1[:, :].bitcast(F16).rearrange("p (a n) -> p a n", a=2)]
        ident = sb("ident", [P, P])
        ident16 = sb("ident16", [P, P], F16)
        ones = sb("ones", [P, P])
        alpha_in = sb("alpha_in", [P, GROUP, P])
        abs_sum = sb("abs_sum", [P, 2 * NW])
        logits = sb("logits", [P, NKEY])
        ex = sb("ex", [P, NKEY])
        prob = sb("prob", [P, 2, NKEY], F16)
        pt = sb("pt", [P, P], F16)
        st1 = sb("st1", [P, NC, 6])
        st2 = sb("st2", [P, NC, 6])
        mv1 = sb("mv1", [P, 2])
        mv2 = sb("mv2", [P, 2])
        ve1 = sb("ve1", [P, 1])
        ve2 = sb("ve2", [P, 1])
        r1 = sb("r1", [P, 1])
        r2 = sb("r2", [P, 1])
        mr1 = sb("mr1", [P, 1])
        mr2 = sb("mr2", [P, 1])
        nm1 = sb("nm1", [P, 1])
        nm2 = sb("nm2", [P, 1])
        neg_half = sb("neg_half", [P, 1])
        eps = sb("eps", [P, 1])
        zero = sb("zero", [P, 1])
        row_max = sb("row_max", [P, 1])
        neg_max = sb("neg_max", [P, 1])
        sum_ex = sb("sum_ex", [P, 1])
        rec_ex = sb("rec_ex", [P, 1])
        coef = sb("coef", [P, 1])
        kmax2 = sb("kmax2", [P, 2])
        kmax = sb("kmax", [P, 1])
        kmax_all = sb("kmax_all", [P, 1])
        kpow = sb("kpow", [P, 1])
        kinv = sb("kinv", [P, 1])
        kscale = sb("kscale", [P, 1])
        lscale = sb("lscale", [P, 1])
        neg_lscale = sb("neg_lscale", [P, 1])
        gates = sb("gates", [P, 2])
        tanh_g = sb("tanh_g", [P, 2])
        gx = sb("gx", [P, 1])
        gy = sb("gy", [P, 1])

        y_ps = psum("y_ps", [P, 2, BANK])
        c_ps = psum("c_ps", [P, 2, BANK])
        s_ps = psum("s_ps", [P, BANK])
        setup_ps = psum("setup_ps", [P, RB, BANK])
        pt_ps = s_ps[:, 2 * P:2 * P + P // 2].bitcast(F16)

        consts_in = sem("consts_in")
        bias_in = sem("bias_in")
        ctx_in = [sem(f"ctx_in{i}") for i in range(2)]
        x_in = [sem(f"x_in{s}") for s in range(RX)]
        out_done = [sem(f"out_done{s}") for s in range(RX)]
        w_in = [sem(f"w_in{s}") for s in range(RW)]
        kts_stored = [sem(f"kts_stored{i}") for i in range(2)]
        khl_stored = [sem(f"khl_stored{i}") for i in range(2)]
        kt_in = sem("kt_in")
        kd_in = sem("kd_in")
        xs1_in = sem("xs1_in")
        moved2 = sem("moved2")
        ones_set = sem("ones_set")
        ident_zero = sem("ident_zero")
        ident_set = sem("ident_set")
        ident16_set = sem("ident16_set")
        small_set = sem("small_set")
        spreader_set = sem("spreader_set")
        kmax2_set = sem("kmax2_set")
        kmax_set = sem("kmax_set")
        kmax_all_set = sem("kmax_all_set")
        kchain = sem("kchain")
        tanh_set = sem("tanh_set")
        gchain = sem("gchain")
        khl_high = sem("khl_high")
        khl_low = sem("khl_low")
        k_tr = sem("k_tr")
        k_high = sem("k_high")
        k_low = sem("k_low")
        w_tr = sem("w_tr")
        w_signed = sem("w_signed")
        abs_dve = sem("abs_dve")
        abs_act = sem("abs_act")
        alpha_in_set = sem("alpha_in_set")
        alpha_tr = sem("alpha_tr")
        alpha_set = sem("alpha_set")
        stats1 = sem("stats1")
        mv1_set = sem("mv1_set")
        ve1_set = sem("ve1_set")
        r1_set = sem("r1_set")
        mr1_set = sem("mr1_set")
        nm1_set = sem("nm1_set")
        factors_set = sem("factors_set")
        spread_full = sem("spread_full")
        spread_set = sem("spread_set")
        xs1_set = sem("xs1_set")
        turned1 = sem("turned1")
        q_high = sem("q_high")
        q_set = sem("q_set")
        scores_ready = sem("scores_ready")
        logits_set = sem("logits_set")
        max_set = sem("max_set")
        neg_max_set = sem("neg_max_set")
        ex_set = sem("ex_set")
        rec_set = sem("rec_set")
        coef_set = sem("coef_set")
        prob_high = sem("prob_high")
        prob_set = sem("prob_set")
        pt_full = sem("pt_full")
        pt_set = sem("pt_set")
        c_ready = sem("c_ready")
        x1_set = sem("x1_set")
        stats2 = sem("stats2")
        mv2_set = sem("mv2_set")
        ve2_set = sem("ve2_set")
        r2_set = sem("r2_set")
        mr2_set = sem("mr2_set")
        nm2_set = sem("nm2_set")
        xn2_set = sem("xn2_set")
        turned2 = sem("turned2")
        x1b_set = sem("x1b_set")
        x1_high = sem("x1_high")
        x1t_set = sem("x1t_set")
        y_ready = sem("y_ready")
        y_scaled = sem("y_scaled")
        y_added = sem("y_added")

        def chunk(n):
            return slice(n * BANK, (n + 1) * BANK)

        def columns(row, h):
            return row.rearrange("p (a h n) -> p h a n", a=4, h=2)[:, h]

        def laid_out(slot, h):
            return xr[:, slot, D // 2 * h:D // 2 * (h + 1)].rearrange("p (a n) -> p a n", a=4)

        def move_to_quadrants(queue, dst, src, moved):
            for a in range(4):
                queue.dma_start(dst[Q * a:Q * (a + 1), :], src[:, chunk(a)]).then_inc(moved, 16)

        def move_x1(queue, u):
            queue.wait_ge(xn2_set, u + 1)
            move_to_quadrants(queue, xs2, xn2, moved2)

        block = ctx.enter_context(nc.Block())

        @block.sync
        def _(sp):
            def load_quadrants(u):
                if not (isinstance(u, int) and u == 0):
                    sp.wait_ge(turned1, u)
                for a in range(4):
                    sp.dma_start(xs1[Q * a:Q * (a + 1), :].rearrange("p (c n) -> p c n", c=4),
                                 x_q[u, a]).then_inc(xs1_in, 16)

            sp.dma_start(gates[:, 0:1], g_xattn.partition_broadcast(P)).then_inc(consts_in, 16)
            sp.dma_start(gates[:, 1:2], g_ffn.partition_broadcast(P)).then_inc(consts_in, 16)
            for i in range(2):
                for h in range(2):
                    sp.dma_start(xr[:, 2 + i, D // 2 * h:D // 2 * (h + 1)].rearrange("p (a n) -> p a n", a=4),
                                 ctx_t[i, h]).then_inc(ctx_in[i], 16)
            sp.dma_start(xr[:, 0, :], x_t[0]).then_inc(x_in[0], 16)
            load_quadrants(0)

            def load_w(h):
                if h >= RW:
                    before = h - RW
                    sp.wait_ge(w_tr, 2 * before + 2)
                    if before % 2 == 0:
                        sp.wait_ge(abs_dve, before // 2 + 1)
                    else:
                        sp.wait_ge(abs_act, before // 2 + 1)
                sp.dma_start(wstage[:, h % RW, :].rearrange("p (a n) -> p a n", a=4),
                             w_t[h // 2, h % 2]).then_inc(w_in[h % RW], 16)

            def load_kt(batch):
                sp.dma_start(kt_cur[:, :, :].rearrange("p a b -> p (a b)"), kt_dram[batch - 1]).then_inc(kt_in, 16)

            def load_kd(batch):
                for c in range(2):
                    sp.dma_start(kd_cur[NKEY * c:NKEY * (c + 1), :, :].rearrange("p a b -> p (a b)"),
                                 kd_dram[batch - 1]).then_inc(kd_in, 16)

            for h in range(RW):
                load_w(h)
                if h == 1:
                    sp.dma_start(xr[:, 1, :], x_t[1]).then_inc(x_in[1], 16)
            sp.wait_ge(k_low, NG)
            sp.dma_start(kt_cur[:, :, :], kts[0][:, 0]).then_inc(kt_in, 16)
            sp.wait_ge(khl_low, 1)
            for c in range(2):
                sp.dma_start(kd_cur[NKEY * c:NKEY * (c + 1), :, :], khl[0][0:NKEY]).then_inc(kd_in, 16)
            load_quadrants(1)
            for h in range(RW, 2 * NW):
                load_w(h)
                if h == BIAS_H:
                    sp.dma_start(bias_b[:, :], bias.partition_broadcast(P)).then_inc(bias_in, 16)
                if h == MOVE0_H:
                    move_x1(sp, 0)
                if h == QUADRANTS2_H:
                    load_quadrants(2)
                if h == MOVE1_H:
                    move_x1(sp, 1)
                if h == X2_H:
                    sp.wait_ge(kts_stored[1], 32)
                    sp.dma_start(xr[:, 2, :], x_t[2]).then_inc(x_in[2], 16)
                if h == X3_H:
                    sp.wait_ge(k_tr, 2 * NG)
                    sp.wait_ge(khl_low, 2)
                    sp.dma_start(xr[:, 3, :], x_t[3]).then_inc(x_in[3], 16)
                if h == QUADRANTS3_H:
                    load_quadrants(3)
            load_quadrants(4)
            move_x1(sp, 2)

            def store(u, r):
                sp.wait_ge(y_added, FINISHED_0 if isinstance(u, int) and u == 0 else u * NC + NC)
                sp.dma_start(out_t[u], xr[:, r, :]).then_inc(out_done[r], 16)

            def reload(u, r, times):
                sp.wait_ge(out_done[r], times * 16)
                sp.dma_start(xr[:, r, :], x_t[u + RX]).then_inc(x_in[r], 16)

            store(0, 0)
            reload(0, 0, 1)
            move_x1(sp, 3)
            store(1, 1)
            reload(1, 1, 1)
            load_quadrants(5)
            store(2, 2)
            move_x1(sp, 4)
            reload(2, 2, 1)
            load_quadrants(6)
            move_x1(sp, 5)

            sp.wait_ge(kts_stored[0], 16)
            sp.wait_ge(kts_stored[1], 32)
            sp.wait_ge(khl_stored[0], 16)
            sp.wait_ge(khl_stored[1], 16 * 2)
            with sp.Fori(0, LOOPS) as i:
                for j in range(STEPS):
                    t, r = i * STEPS + (FIRST + j), (FIRST + j) % RX
                    store(t - 1, (r - 1) % RX)
                    reload(t - 1, (r - 1) % RX, i + (FIRST + j - 1) // RX + 1)
                    load_quadrants(t + 3)
                    if j == 1:
                        batch = (i + 2) // 2
                        sp.wait_ge(scores_ready, i * STEPS + 2 * STEPS)
                        load_kt(batch)
                        sp.wait_ge(c_ready, i * STEPS * NC + 2 * STEPS * NC)
                        load_kd(batch)
                    move_x1(sp, t + 2)
            for t in range(FIRST + STEPS * LOOPS, NT):
                store(t - 1, (t - 1) % RX)
                if t + 3 < NT:
                    reload(t - 1, (t - 1) % RX, (t - 1) // RX + 1)
                    load_quadrants(t + 3)
                if t + 2 < NT:
                    move_x1(sp, t + 2)
            for n in range(NC):
                sp.wait_ge(y_added, (NT - 1) * NC + n + 1)
                sp.dma_start(out_t[NT - 1][:, chunk(n)], xr[:, (NT - 1) % RX, chunk(n)]).then_inc(out_done[(NT - 1) % RX], 16)
            for r in range(RX):
                sp.wait_ge(out_done[r], 16 * (NT // RX + (NC - 1 if r == (NT - 1) % RX else 0)))

        @block.gpsimd
        def _(pool):
            nc.gpsimd.memset(ident[:, :], 0.0).then_inc(ident_zero, 1)
            pool.wait_ge(ident_zero, 1)
            nc.gpsimd.affine_select(out=ident[:, :], in_=ident[:, :], compare_op=ALU.not_equal, fill=1.0, base=0,
                                    pattern=[[-1, P]], channel_multiplier=1).then_inc(ident_set, 1)
            nc.gpsimd.memset(neg_half[:, :], -0.5).then_inc(small_set, 1)
            nc.gpsimd.memset(eps[:, :], EPS).then_inc(small_set, 1)
            nc.gpsimd.memset(zero[:, :], 0.0).then_inc(small_set, 1)
            pool.wait_ge(small_set, 3)

            def rstd(u, mv, ve, r, mr, nm, mv_set, ve_set, r_set, mr_set, nm_set):
                pool.wait_ge(mv_set, u + 1)
                nc.gpsimd.tensor_tensor(ve[:, :], mv[:, 1:2], eps[:, :], ALU.add).then_inc(ve_set, 1)
                pool.wait_ge(ve_set, u + 1)
                nc.gpsimd.tensor_tensor(r[:, :], ve[:, :], neg_half[:, :], ALU.pow).then_inc(r_set, 1)
                pool.wait_ge(r_set, u + 1)
                nc.gpsimd.tensor_tensor(mr[:, :], mv[:, 0:1], r[:, :], ALU.mult).then_inc(mr_set, 1)
                pool.wait_ge(mr_set, u + 1)
                nc.gpsimd.tensor_tensor(nm[:, :], zero[:, :], mr[:, :], ALU.subtract).then_inc(nm_set, 1)

            def rstd1(u):
                rstd(u, mv1, ve1, r1, mr1, nm1, mv1_set, ve1_set, r1_set, mr1_set, nm1_set)

            def rstd2(u):
                rstd(u, mv2, ve2, r2, mr2, nm2, mv2_set, ve2_set, r2_set, mr2_set, nm2_set)

            def add_bias(u, r):
                pool.wait_ge(xn2_set, u + 1)
                nc.gpsimd.tensor_tensor(xr[:, r, :], xr[:, r, :], bias_b[:, :], ALU.add).then_inc(x1b_set, 1)

            pool.wait_ge(kmax_set, 1)
            nc.gpsimd.partition_all_reduce(kmax_all[:, :], kmax[:, :], P, bass.bass_isa.ReduceOp.max).then_inc(kmax_all_set, 1)
            rstd1(0)
            def store_kt(i):
                pool.wait_ge(k_low, NG * (i + 1))
                for b in range(2):
                    if 2 * i + b > 0:
                        pool.dma_start(kt_dram[2 * i + b - 1].rearrange("p (a k) -> p a k", a=ND),
                                       kts[i][:, b]).then_inc(kts_stored[i], 16)

            def store_kd(i):
                pool.wait_ge(khl_low, i + 1)
                for b in range(2):
                    if 2 * i + b > 0:
                        pool.dma_start(kd_dram[2 * i + b - 1],
                                       khl[i][NKEY * b:NKEY * (b + 1)].rearrange("p a b -> p (a b)")).then_inc(khl_stored[i], 16)

            store_kt(0)
            store_kd(0)
            rstd1(1)
            rstd2(0)
            pool.wait_ge(gchain, 3)
            add_bias(0, 0)
            rstd2(1)
            add_bias(1, 1)
            store_kt(1)
            store_kd(1)
            rstd1(2)
            rstd1(3)
            rstd2(2)
            add_bias(2, 2)
            rstd2(3)
            rstd1(4)
            add_bias(3, 3)
            rstd1(5)
            rstd2(4)
            add_bias(4, 0)

            def step(t, r, attention=True, ln1=True):
                if ln1:
                    rstd1(t + 3)
                if attention:
                    rstd2(t + 2)
                    add_bias(t + 2, (r + 2) % RX)

            step(3, 3)
            with pool.Fori(0, LOOPS) as i:
                for j in range(STEPS):
                    step(i * STEPS + (FIRST + j), (FIRST + j) % RX)
            for t in range(FIRST + STEPS * LOOPS, NT):
                step(t, t % RX, attention=t + 2 < NT, ln1=t + 3 < NT)

        @block.scalar
        def _(act):
            def normalise1(u):
                act.wait_ge(spread_full, u + 1)
                nc.scalar.copy(spread[:, :, :].rearrange("p a b -> p (a b)"), s_ps[:, 0:8]).then_inc(spread_set, 1)
                act.wait_ge(spread_set, u + 1)
                act.wait_ge(xs1_in, u * 64 + 64)
                for c in range(4):
                    last = nc.scalar.activation(xs1[:, chunk(c)], xs1[:, chunk(c)], ACT.Identity,
                                                bias=spread[:, 1, c:c + 1], scale=spread[:, 0, c:c + 1])
                last.then_inc(xs1_set, 1)

            def normalise2(u, r):
                act.wait_ge(nm2_set, u + 1)
                if not (isinstance(u, int) and u == 0):
                    act.wait_ge(x1t_set, u)
                nc.scalar.activation(xn2[:, :], xr[:, r, :], ACT.Identity, bias=nm2[:, :],
                                     scale=r2[:, :]).then_inc(xn2_set, 1)

            def high_q(u):
                act.wait_ge(turned1, u + 1)
                if not (isinstance(u, int) and u == 0):
                    act.wait_ge(scores_ready, u)
                nc.scalar.activation(qt[:, 0, :], xn1[:, :], ACT.Copy, scale=LN_SCALE).then_inc(q_high, 1)

            def high_x1(u, slot):
                act.wait_ge(turned2, u + 1)
                if not isinstance(u, int) or u >= 3:
                    act.wait_ge(y_ready, u * NC - NC)
                elif u == 2:
                    act.wait_ge(y_ready, FINISHED_0)
                nc.scalar.activation(x1t[:, slot, 0, :], xn2[:, :], ACT.Copy, scale=LN_SCALE).then_inc(x1_high, 1)

            def exp(u):
                act.wait_ge(neg_max_set, u + 1)
                nc.scalar.activation(ex[:, :], logits[:, :], ACT.Exp, bias=neg_max[:, :], scale=lscale[:, :],
                                     accum_out=sum_ex[:, :]).then_inc(ex_set, 1)

            def copy_pt(u):
                if not (isinstance(u, int) and u == 0):
                    act.wait_ge(c_ready, u * NC)
                act.wait_ge(pt_full, u + 1)
                nc.scalar.copy(pt[:, :], pt_ps).then_inc(pt_set, 1)

            def sign_group(m):
                w, g = m // NG, m % NG
                act.wait_ge(w_tr, m + 1)
                nc.scalar.activation(wsign[:, GROUP * g:GROUP * (g + 1), P * w:P * (w + 1)],
                                     setup_ps[:, setup_order.index(("w", m)) % RB, :].rearrange("p (a b) -> p a b", a=GROUP),
                                     ACT.Sign).then_inc(w_signed, 1)

            def abs_half(h):
                act.wait_ge(w_in[h % RW], 16 * (h // RW + 1))
                act.wait_ge(w_tr, 2 * h + 2)
                nc.scalar.activation(wstage[:, h % RW, :], wstage[:, h % RW, :], ACT.Abs,
                                     accum_out=abs_sum[:, h:h + 1]).then_inc(abs_act, 1)

            def sign_groups(groups):
                for m in groups:
                    sign_group(m)
                    if m % NG == NG - 1:
                        abs_half(2 * (m // NG) + 1)

            def key_high(i, g):
                act.wait_ge(k_tr, NG * i + g + 1)
                src = setup_ps[:, setup_order.index(("keys", NG * i + g)) % RB, :].rearrange(
                    "p (a b k) -> p b a k", a=GROUP, b=2)
                for b in range(2):
                    last = nc.scalar.activation(kts[i][:, b, GROUP * g:GROUP * (g + 1), 0:NKEY], src[:, b], ACT.Copy,
                                                scale=kscale[:, :])
                last.then_inc(k_high, 1)

            def khl_high_part(i):
                act.wait_ge(ctx_in[i], 32)
                for h in range(2):
                    last = nc.scalar.activation(columns(khl[i][:, 0, :], h), laid_out(2 + i, h), ACT.Copy,
                                                scale=kscale[:, :])
                last.then_inc(khl_high, 1)

            act.wait_ge(consts_in, 32)
            nc.scalar.activation(tanh_g[:, :], gates[:, :], ACT.Tanh).then_inc(tanh_set, 1)
            act.wait_ge(kchain, 4)
            for g in range(NG):
                key_high(0, g)
            normalise1(0)
            khl_high_part(0)
            high_q(0)
            sign_groups(range(8))
            exp(0)
            copy_pt(0)
            normalise1(1)
            sign_groups(range(8, 12))
            act.wait_ge(kts_stored[0], 16)
            act.wait_ge(kt_in, 16)
            normalise2(0, 0)
            high_q(1)
            sign_groups(range(12, 16))
            act.wait_ge(khl_stored[0], 16)
            act.wait_ge(kd_in, 32)
            high_x1(0, 0)
            exp(1)
            sign_groups(range(16, 18))
            copy_pt(1)
            sign_groups(range(18, BEFORE_W))

            for k in range(PAIR_BLOCKS):
                sign_groups(pair_w[k])
                if k == NORM2_1:
                    normalise2(1, 1)
                for g in PAIR_KEYS.get(k, ()):
                    key_high(1, g)
                if k == TURN_X1_1:
                    high_x1(1, 1)
                if k == PAIR_KEY_ROWS:
                    act.wait_ge(q_set, 2)
                    khl_high_part(1)
                if k in PAIR_SPREAD:
                    normalise1(PAIR_SPREAD[k])
                if k in PAIR_SPLIT:
                    high_q(PAIR_SPLIT[k])
                if k in PAIR_SCORES:
                    exp(PAIR_SCORES[k])
                if k in PAIR_PT:
                    copy_pt(PAIR_PT[k])
                if k == NORM2_2:
                    normalise2(2, 2)
                if k == LOW_X1_2:
                    high_x1(2, 0)
            normalise2(3, 3)

            normalise1(4)
            high_q(4)
            high_x1(3, 1)
            exp(4)
            copy_pt(4)
            normalise1(5)
            high_q(5)
            normalise2(4, 0)

            def step(t, r, x1=True, attention=True, ln1=True, late=False):
                if x1 and not late:
                    high_x1(t + 1, (r + 1) % 2)
                if attention:
                    exp(t + 2)
                    copy_pt(t + 2)
                if late:
                    high_x1(t + 1, (r + 1) % 2)
                if ln1:
                    normalise1(t + 3)
                if attention:
                    normalise2(t + 2, (r + 2) % RX)
                if ln1:
                    high_q(t + 3)

            step(3, 3, late=True)
            with act.Fori(0, LOOPS) as i:
                for j in range(STEPS):
                    step(i * STEPS + (FIRST + j), (FIRST + j) % RX)
            for t in range(FIRST + STEPS * LOOPS, NT):
                step(t, t % RX, x1=t + 1 < NT, attention=t + 2 < NT, ln1=t + 3 < NT)

        @block.vector
        def _(dve):
            def norm_stats1(u, r, n):
                if n == 0:
                    dve.wait_ge(x_in[r], (u - r) * (16 // RX) + 16)
                nc.vector.bn_stats(st1[:, n, :], xr[:, r, chunk(n)]).then_inc(stats1, 1)

            def stats1_done(u):
                dve.wait_ge(stats1, u * NC + NC)

            def norm_mean1(u):
                nc.vector.bn_aggr(mv1[:, :], st1[:, :, :].rearrange("p a b -> p (a b)")).then_inc(mv1_set, 1)

            def stats2_done(u):
                dve.wait_ge(stats2, u * NC + NC)

            def norm_mean2(u):
                nc.vector.bn_aggr(mv2[:, :], st2[:, :, :].rearrange("p a b -> p (a b)")).then_inc(mv2_set, 1)

            def ln1_mean(u, r):
                for n in range(NC):
                    norm_stats1(u, r, n)
                stats1_done(u)
                norm_mean1(u)

            def turn(dst, src):
                for h in range(2):
                    last = nc.vector.transpose(
                        dst[:, D // 2 * h:D // 2 * (h + 1)].rearrange("p (k i c) -> p k c i", k=8, c=4),
                        src[:, :].rearrange("p (c h j k) -> p h k c j", c=4, h=2, j=Q)[:, h])
                return last

            def place_factors(u):
                dve.wait_ge(nm1_set, u + 1)
                nc.vector.tensor_scalar(factors[:, 0, :], own_c[:, :], r1[:, 0:1], None, ALU.mult)
                nc.vector.tensor_scalar(factors[:, 1, :], own_c[:, :], nm1[:, 0:1], None, ALU.mult).then_inc(factors_set, 1)

            def turn_q(u):
                dve.wait_ge(xs1_set, u + 1)
                turn(xn1, xs1).then_inc(turned1, 1)

            def turn_x1(u):
                dve.wait_ge(moved2, u * 64 + 64)
                turn(xn2, xs2).then_inc(turned2, 1)

            def low_q(u):
                dve.wait_ge(q_high, u + 1)
                nc.vector.scalar_tensor_tensor(out=qt[:, 1, :], in0=xn1[:, :], scalar=LN_SCALE, in1=qt[:, 0, :],
                                               op0=ALU.mult, op1=ALU.subtract).then_inc(q_set, 1)

            def low_x1(u, slot):
                dve.wait_ge(x1_high, u + 1)
                nc.vector.scalar_tensor_tensor(out=x1t[:, slot, 1, :], in0=xn2[:, :], scalar=LN_SCALE,
                                               in1=x1t[:, slot, 0, :], op0=ALU.mult, op1=ALU.subtract).then_inc(x1t_set, 1)

            def max_logits(u):
                dve.wait_ge(scores_ready, u + 1)
                nc.vector.tensor_reduce(logits[:, :], s_ps[:, 0:P].rearrange("p (h k) -> p k h", h=2), X,
                                        ALU.add).then_inc(logits_set, 1)
                dve.wait_ge(logits_set, u + 1)
                nc.vector.tensor_reduce(row_max[:, :], logits[:, :], X, ALU.max).then_inc(max_set, 1)
                dve.wait_ge(max_set, u + 1)
                nc.vector.tensor_scalar(neg_max[:, :], row_max[:, :], neg_lscale[:, 0:1], None,
                                        ALU.mult).then_inc(neg_max_set, 1)

            def split_probs(u):
                dve.wait_ge(ex_set, u + 1)
                nc.vector.tensor_scalar(prob[:, 0, :], ex[:, :], PROB_SCALE, None, ALU.mult).then_inc(prob_high, 1)
                nc.vector.reciprocal(rec_ex[:, :], sum_ex[:, :]).then_inc(rec_set, 1)
                dve.wait_ge(prob_high, u + 1)
                nc.vector.scalar_tensor_tensor(out=prob[:, 1, :], in0=ex[:, :], scalar=PROB_SCALE, in1=prob[:, 0, :],
                                               op0=ALU.mult, op1=ALU.subtract).then_inc(prob_set, 1)
                dve.wait_ge(rec_set, u + 1)
                nc.vector.tensor_scalar(coef[:, :], rec_ex[:, :], gx[:, 0:1], None, ALU.mult).then_inc(coef_set, 1)

            def add_attention(u, r, n):
                dve.wait_ge(c_ready, u * NC + (n + 1))
                if n == 0:
                    dve.wait_ge(coef_set, u + 1)
                nc.vector.scalar_tensor_tensor(out=xr[:, r, chunk(n)], in0=c_ps[:, n % 2, :], scalar=coef[:, 0:1],
                                               in1=xr[:, r, chunk(n)], op0=ALU.mult, op1=ALU.add).then_inc(x1_set, 1)

            def norm_stats2(u, r, n):
                dve.wait_ge(x1_set, u * NC + (n + 1))
                nc.vector.bn_stats(st2[:, n, :], xr[:, r, chunk(n)]).then_inc(stats2, 1)

            def scale_y(t, n, r):
                k = seq_y(t, n)
                bank = (k if isinstance(k, int) else n) % 2
                dve.wait_ge(y_ready, k + 1)
                nc.vector.tensor_tensor(ytmp[:, bank, :], y_ps[:, bank, :], alpha_b[:, chunk(n)],
                                        ALU.mult).then_inc(y_scaled, 1)

            def add_y(t, n, r):
                k = seq_y(t, n)
                bank = (k if isinstance(k, int) else n) % 2
                dve.wait_ge(y_scaled, k + 1)
                dve.wait_ge(x1b_set, t + 1)
                nc.vector.tensor_tensor(xr[:, r, chunk(n)], ytmp[:, bank, :], xr[:, r, chunk(n)],
                                        ALU.add).then_inc(y_added, 1)

            def finish_y(t, n, r):
                scale_y(t, n, r)
                add_y(t, n, r)

            def sum_abs(w):
                h = 2 * w
                dve.wait_ge(w_in[h % RW], 16 * (h // RW + 1))
                nc.vector.tensor_reduce(abs_sum[:, h:h + 1], wstage[:, h % RW, :], X, ALU.add,
                                        apply_absolute_value=True).then_inc(abs_dve, 1)

            def spread_alpha(w):
                dve.wait_ge(abs_dve, w + 1)
                dve.wait_ge(abs_act, w + 1)
                if w >= GROUP:
                    dve.wait_ge(alpha_tr, w // GROUP)
                nc.vector.tensor_scalar(alpha_in[:, w % GROUP, :], ones[:, :], abs_sum[:, 2 * w:2 * w + 1],
                                        abs_sum[:, 2 * w + 1:2 * w + 2], ALU.mult, ALU.add).then_inc(alpha_in_set, 1)

            def take_alpha(n):
                dve.wait_ge(alpha_tr, n + 1)
                nc.vector.tensor_scalar(alpha_b[:, chunk(n)], setup_ps[:, setup_order.index(("alpha", n)) % RB, :],
                                        gy[:, 0:1], None, ALU.mult).then_inc(alpha_set, 1)

            def key_low(i, g):
                dve.wait_ge(k_high, NG * i + g + 1)
                src = setup_ps[:, setup_order.index(("keys", NG * i + g)) % RB, :].rearrange(
                    "p (a b k) -> p b a k", a=GROUP, b=2)
                for b in range(2):
                    dst = kts[i][:, b, GROUP * g:GROUP * (g + 1), :]
                    last = nc.vector.scalar_tensor_tensor(out=dst[:, :, NKEY:], in0=src[:, b], scalar=kscale[:, 0:1],
                                                          in1=dst[:, :, 0:NKEY], op0=ALU.mult, op1=ALU.subtract)
                last.then_inc(k_low, 1)

            def khl_low_part(i):
                dve.wait_ge(khl_high, i + 1)
                for h in range(2):
                    last = nc.vector.scalar_tensor_tensor(
                        out=columns(khl[i][:, 1, :], h), in0=laid_out(2 + i, h), scalar=kscale[:, 0:1],
                        in1=columns(khl[i][:, 0, :], h), op0=ALU.mult, op1=ALU.subtract)
                last.then_inc(khl_low, 1)

            nc.vector.memset(ones[:, :], 1.0).then_inc(ones_set, 1)
            dve.wait_ge(ident_set, 1)
            nc.vector.tensor_reduce(own_c[:, :], ident[:, :].rearrange("p (i c) -> p c i", c=4), X,
                                    ALU.add).then_inc(spreader_set, 1)
            for a in range(4):
                nc.vector.tensor_reduce(same_i[:, Q * a:Q * (a + 1)], ident[:, :].rearrange("p (i c) -> p i c", c=4), X,
                                        ALU.add).then_inc(spreader_set, 1)
            nc.vector.tensor_copy(ident16[:, :], ident[:, :]).then_inc(ident16_set, 1)
            dve.wait_ge(spreader_set, 5)
            for i in range(2):
                dve.wait_ge(ctx_in[i], 32)
                nc.vector.tensor_reduce(kmax2[:, i:i + 1], xr[:, 2 + i, :], X, ALU.max,
                                        apply_absolute_value=True).then_inc(kmax2_set, 1)
            dve.wait_ge(kmax2_set, 2)
            nc.vector.tensor_reduce(kmax[:, :], kmax2[:, :], X, ALU.max).then_inc(kmax_set, 1)
            dve.wait_ge(kmax_all_set, 1)
            nc.vector.tensor_scalar(kpow[:, :].bitcast(I32), kmax_all[:, :].bitcast(I32), 0x7F800000, None,
                                    ALU.bitwise_and).then_inc(kchain, 1)
            dve.wait_ge(kchain, 1)
            nc.vector.tensor_scalar(kinv[:, :], kpow[:, :], 2.0 ** -90, 1.0 / KEY_TOP, ALU.max, ALU.mult).then_inc(kchain, 1)
            dve.wait_ge(kchain, 2)
            nc.vector.reciprocal(kscale[:, :], kinv[:, :]).then_inc(kchain, 1)
            dve.wait_ge(kchain, 3)
            nc.vector.tensor_scalar(lscale[:, :], kinv[:, :], 1.0 / LN_SCALE, None, ALU.mult).then_inc(kchain, 1)
            nc.vector.tensor_scalar(neg_lscale[:, :], kinv[:, :], -1.0 / LN_SCALE, None, ALU.mult).then_inc(kchain, 1)
            dve.wait_ge(tanh_set, 1)
            nc.vector.tensor_scalar(gx[:, :], tanh_g[:, 0:1], kinv[:, 0:1], 1.0 / PROB_SCALE, ALU.mult,
                                    ALU.mult).then_inc(gchain, 1)
            nc.vector.tensor_scalar(gy[:, :], tanh_g[:, 1:2], 1.0 / (D * LN_SCALE), None, ALU.mult).then_inc(gchain, 1)
            dve.wait_ge(kchain, 5)
            dve.wait_ge(gchain, 2)
            ln1_mean(0, 0)
            key_low(0, 0)
            place_factors(0)
            for g in range(1, NG):
                key_low(0, g)
            turn_q(0)
            khl_low_part(0)
            low_q(0)
            ln1_mean(1, 1)
            sum_abs(0)
            place_factors(1)
            sum_abs(1)
            max_logits(0)
            split_probs(0)
            for n in range(NC):
                add_attention(0, 0, n)
                norm_stats2(0, 0, n)
            stats2_done(0)
            norm_mean2(0)
            sum_abs(2)
            turn_q(1)
            dve.wait_ge(bias_in, 16)
            nc.vector.tensor_scalar(bias_b[:, :], bias_b[:, :], tanh_g[:, 1:2], None, ALU.mult).then_inc(gchain, 1)
            low_q(1)
            sum_abs(3)
            turn_x1(0)
            max_logits(1)
            sum_abs(4)
            split_probs(1)
            low_x1(0, 0)
            add_attention(1, 1, 0)
            norm_stats2(1, 1, 0)
            add_attention(1, 1, 1)
            norm_stats2(1, 1, 1)
            for n in range(2, NC):
                add_attention(1, 1, n)
                norm_stats2(1, 1, n)
            stats2_done(1)
            norm_mean2(1)
            sum_abs(5)
            dve.wait_ge(ones_set, 1)
            for w in range(GROUP):
                spread_alpha(w)

            for k in range(PAIR_BLOCKS):
                if k - 1 in PAIR_ALPHA:
                    take_alpha(PAIR_ALPHA[k - 1])
                for m in pair_w[k]:
                    if m % NG == 0 and m > BEFORE_W:
                        sum_abs(m // NG)
                if k == 1:
                    spread_alpha(BEFORE_W // NG - 1)
                if k == TURN_X1_1:
                    turn_x1(1)
                for g in PAIR_KEYS.get(k, ()):
                    key_low(1, g)
                if k == LOW_X1_1:
                    low_x1(1, 1)
                if k == PAIR_KEY_ROWS:
                    khl_low_part(1)
                for m in pair_w[k]:
                    if m % NG == NG - 1:
                        spread_alpha(m // NG)
                if k in PAIR_STATS:
                    ln1_mean(PAIR_STATS[k], PAIR_STATS[k])
                if k in PAIR_PLACE:
                    place_factors(PAIR_PLACE[k])
                if k in PAIR_TURN:
                    if PAIR_TURN[k] == 2:
                        dve.wait_ge(khl_stored[1], 16 * 2)
                    turn_q(PAIR_TURN[k])
                if k in PAIR_SPLIT:
                    low_q(PAIR_SPLIT[k])
                if k in PAIR_SCORES:
                    max_logits(PAIR_SCORES[k])
                    split_probs(PAIR_SCORES[k])
                if k in PAIR_C:
                    u, n = PAIR_C[k]
                    add_attention(u, u, n)
                    norm_stats2(u, u, n)
                    if n == NC - 1:
                        stats2_done(u)
                        norm_mean2(u)
                if k % 4 == 3 and k < 31:
                    t, n = PAIR_ORDER[k // 4]
                    if t == 0:
                        dve.wait_ge(alpha_set, n + 1)
                    finish_y(t, n, t)
                if k == TURN_X1_2:
                    turn_x1(2)
                if k == LOW_X1_2:
                    low_x1(2, 0)

            finish_y(*PAIR_ORDER[7], 1)
            ln1_mean(4, 0)
            finish_y(2, 0, 2)
            place_factors(4)
            turn_q(4)
            turn_x1(3)
            low_q(4)
            finish_y(2, 1, 2)
            low_x1(3, 1)
            max_logits(4)
            split_probs(4)
            ln1_mean(5, 1)
            place_factors(5)
            finish_y(2, 2, 2)
            for n in range(NC):
                add_attention(4, 0, n)
                norm_stats2(4, 0, n)
                if n == 2:
                    turn_q(5)
            stats2_done(4)
            norm_mean2(4)
            low_q(5)

            def step(t, r, x1=True, attention=True, ln1=True):
                a, ra = t + 2, (r + 2) % RX
                a1, ra1 = t + 3, (r + 3) % RX
                finish_y(t - 1, 3, (r - 1) % RX)
                if x1:
                    turn_x1(t + 1)
                if attention:
                    max_logits(a)
                    split_probs(a)
                if x1:
                    low_x1(t + 1, (r + 1) % 2)
                if ln1:
                    for n in range(NC):
                        norm_stats1(a1, ra1, n)
                    stats1_done(a1)
                scale_y(t, 0, r)
                if ln1:
                    norm_mean1(a1)
                add_y(t, 0, r)
                for n in range(NC):
                    if attention:
                        add_attention(a, ra, n)
                        norm_stats2(a, ra, n)
                    if ln1 and n == 0:
                        place_factors(a1)
                if attention:
                    stats2_done(a)
                scale_y(t, 1, r)
                if attention:
                    norm_mean2(a)
                add_y(t, 1, r)
                if ln1:
                    turn_q(a1)
                finish_y(t, 2, r)
                if ln1:
                    low_q(a1)

            finish_y(2, 3, 2)
            max_logits(5)
            split_probs(5)
            finish_y(3, 0, 3)
            turn_x1(4)
            add_attention(5, 1, 0)
            norm_stats2(5, 1, 0)
            ln1_mean(6, 2)
            add_attention(5, 1, 1)
            norm_stats2(5, 1, 1)
            place_factors(6)
            add_attention(5, 1, 2)
            norm_stats2(5, 1, 2)
            low_x1(4, 0)
            add_attention(5, 1, 3)
            norm_stats2(5, 1, 3)
            stats2_done(5)
            norm_mean2(5)
            finish_y(3, 1, 3)
            turn_q(6)
            finish_y(3, 2, 3)
            low_q(6)

            with dve.Fori(0, LOOPS) as i:
                for j in range(STEPS):
                    step(i * STEPS + (FIRST + j), (FIRST + j) % RX)
            for t in range(FIRST + STEPS * LOOPS, NT):
                step(t, t % RX, x1=t + 1 < NT, attention=t + 2 < NT, ln1=t + 3 < NT)
            finish_y(NT - 1, 3, (NT - 1) % RX)

        @block.tensor
        def _(pe):
            def through_bank(kind, src, done):
                n = setup_order.index(kind)
                if n >= RB:
                    what, m = setup_order[n - RB]
                    pe.wait_ge({"keys": k_low, "w": w_signed, "alpha": alpha_set}[what], m + 1)
                for b in range(GROUP):
                    last = nc.tensor.transpose(setup_ps[:, n % RB, P * b:P * (b + 1)], src(b), ident[:, :])
                last.then_inc(done, 1)

            def transpose_keys(i, g):
                if g == 0:
                    pe.wait_ge(ctx_in[i], 32)
                rows = xr[:, 2 + i, D // 2 * (g // 2):D // 2 * (g // 2 + 1)].rearrange("p (m k) -> p k m", k=8)
                through_bank(("keys", NG * i + g), lambda b: rows[:, GROUP * (g % 2) + b], k_tr)

            def transpose_w(m):
                h = m // 2
                if m % 2 == 0:
                    pe.wait_ge(w_in[h % RW], 16 * (h // RW + 1))
                rows = wstage[:, h % RW, :].rearrange("p (m k) -> p k m", k=8)
                through_bank(("w", m), lambda b: rows[:, GROUP * (m % 2) + b], w_tr)

            def transpose_alpha(n):
                pe.wait_ge(alpha_in_set, GROUP * (n + 1))
                through_bank(("alpha", n), lambda b: alpha_in[:, b, :], alpha_tr)

            def spread_factors(u):
                if isinstance(u, int) and u == 0:
                    pe.wait_ge(spreader_set, 5)
                pe.wait_ge(factors_set, u + 1)
                nc.tensor.matmul(s_ps[:, 0:8], same_i[:, :], factors[:, :, :].rearrange("p a b -> p (a b)"), start=True,
                                 stop=True).then_inc(spread_full, 1)

            def scores(u):
                pe.wait_ge(q_set, u + 1)
                for k in range(ND):
                    for part in range(2):
                        last = nc.tensor.matmul(s_ps[:, 0:P], qt[:, part, P * k:P * (k + 1)], kt_cur[:, k, :],
                                                start=(k == 0 and part == 0), stop=(k == ND - 1 and part == 1))
                last.then_inc(scores_ready, 1)

            def transpose_probs(u):
                pe.wait_ge(prob_set, u + 1)
                nc.tensor.transpose(pt_ps, prob[:, :, :].rearrange("p a b -> p (a b)"), ident16[:, :]).then_inc(pt_full, 1)

            def attend(u, n):
                if n == 0:
                    pe.wait_ge(pt_set, u + 1)
                if not (isinstance(u, int) and u == 0 and n < 2):
                    pe.wait_ge(x1_set, u * NC + (n - 1))
                for part in range(2):
                    last = nc.tensor.matmul(c_ps[:, n % 2, :], pt[:, :], kd_cur[:, part, chunk(n)],
                                            start=(part == 0), stop=(part == 1))
                last.then_inc(c_ready, 1)

            def ffn_block(bank, slot, n, q):
                for k in range(4 * q, 4 * q + 4):
                    for part in range(2):
                        last = nc.tensor.matmul(y_ps[:, bank, :], x1t[:, slot, part, P * k:P * (k + 1)],
                                                wsign[:, k, chunk(n)], start=(k == 0 and part == 0),
                                                stop=(k == ND - 1 and part == 1))
                if q == 3:
                    last.then_inc(y_ready, 1)

            pe.wait_ge(ident_set, 1)
            for g in range(NG):
                transpose_keys(0, g)
            spread_factors(0)
            for m in range(8):
                transpose_w(m)
            pe.wait_ge(kt_in, 16)
            pe.wait_ge(spread_set, 1)
            scores(0)
            pe.wait_ge(ident16_set, 1)
            transpose_probs(0)
            pe.wait_ge(pt_set, 1)
            spread_factors(1)
            pe.wait_ge(kd_in, 32)
            for n in range(NC):
                attend(0, n)
                transpose_w(8 + n)
            for m in range(12, 16):
                transpose_w(m)
            pe.wait_ge(spread_set, 2)
            scores(1)
            transpose_w(16)
            transpose_w(17)
            transpose_probs(1)
            attend(1, 0)
            transpose_w(18)
            attend(1, 1)
            transpose_w(19)

            for k in range(PAIR_BLOCKS):
                (tile, n), q = PAIR_ORDER[k // 4], k % 4
                if q == 0:
                    if tile == 0:
                        pe.wait_ge(w_signed, CHUNK_GROUPS * (n + 1))
                    if n == 0:
                        pe.wait_ge(x1t_set, tile + 1)
                    if k >= 8:
                        pe.wait_ge(y_scaled, k // 4 - 1)
                ffn_block(k // 4 % 2, tile, n, q)
                if k == 0:
                    attend(1, 2)
                    attend(1, 3)
                for m in pair_w[k]:
                    transpose_w(m)
                for g in PAIR_KEYS.get(k, ()):
                    transpose_keys(1, g)
                if k in PAIR_ALPHA:
                    transpose_alpha(PAIR_ALPHA[k])
                if k in PAIR_SCORES:
                    scores(PAIR_SCORES[k])
                if k in PAIR_PT:
                    transpose_probs(PAIR_PT[k])
                if k in PAIR_C:
                    attend(*PAIR_C[k])
                if k in PAIR_SPREAD:
                    spread_factors(PAIR_SPREAD[k])

            def step(t, r, attention=True, ln1=True, keys=None, late=False, spread_at=SPREAD_AT):
                scores_at, pt_at, c_at = (LATE_SCORES_AT, LATE_PT_AT, LATE_C_AT) if late else (SCORES_AT, PT_AT, C_AT)
                pe.wait_ge(x1t_set, t + 1)
                for k in range(BLOCKS):
                    n, q = k // 4, k % 4
                    if q == 0:
                        pe.wait_ge(y_scaled, t * NC + (n - 1))
                    ffn_block(n % 2, r % 2, n, q)
                    if late and k == LATE_FIRST_SPREAD_AT:
                        spread_factors(t + 2)
                    if ln1 and k == spread_at:
                        spread_factors(t + 3)
                    if attention:
                        if k == scores_at:
                            if keys is not None:
                                pe.wait_ge(kt_in, keys)
                            scores(t + 2)
                        if k == pt_at:
                            transpose_probs(t + 2)
                        if k in c_at:
                            if c_at[k] == 0 and keys is not None:
                                pe.wait_ge(kd_in, 2 * keys)
                            attend(t + 2, c_at[k])

            step(2, 2, late=True, spread_at=LATE_SPREAD_AT)
            step(3, 3, spread_at=STEP3_SPREAD_AT)
            with pe.Fori(0, LOOPS) as i:
                for j in range(STEPS):
                    step(i * STEPS + (FIRST + j), (FIRST + j) % RX, keys=i * 16 + 32 if j == 2 else None)
            for t in range(FIRST + STEPS * LOOPS, NT):
                step(t, t % RX, attention=t + 2 < NT, ln1=t + 3 < NT)


_INS = ['x', 'ctx_4096', 'g_xattn', 'g_ffn', 'L0_ffn_weight_real', 'L0_ffn_bias']
_OUTS = [((4, 1024, 2048), 'float32')]


def kernel(**inputs):
    import numpy as _np
    import concourse.bacc as _bacc
    from concourse import mybir as _mybir
    from concourse.bass_utils import run_bass_kernel_spmd as _run

    nc = _bacc.Bacc("TRN2", target_bir_lowering=False, num_devices=1)
    arrays, args = {}, []
    for name in _INS:
        a = _np.ascontiguousarray(inputs[name])
        arrays[f"in_{name}_dram"] = a
        args.append(nc.dram_tensor(f"in_{name}_dram", a.shape, _mybir.dt.from_np(a.dtype), kind="ExternalInput").ap())
    for i, (shape, dtype) in enumerate(_OUTS):
        dt = _mybir.dt.from_np(_np.dtype(dtype))
        args.append(nc.dram_tensor(f"out_{i}_dram", shape, dt, kind="ExternalOutput").ap())
    flamingo_gated_kernel(nc, *args)
    r = _run(nc, [arrays], core_ids=[0])
    got = tuple(r.results[0][f"out_{i}_dram"] for i in range(len(_OUTS)))
    return got[0]
```
